# Optimizing a Trainium2 kernel written in Bass

```python
import numpy as np
import jax
import jax.numpy as jnp

def _softmax(x, axis=-1):
    return jax.nn.softmax(x, axis=axis)

def _gelu(x):
    return jax.nn.gelu(x, approximate=True)

def _silu(x):
    return jax.nn.silu(x)

def _sigmoid(x):
    return jax.nn.sigmoid(x)

def _layernorm(x, axis=-1, eps=1e-05):
    m = jnp.mean(x, axis=axis, keepdims=True)
    v = jnp.var(x, axis=axis, keepdims=True)
    return (x - m) / jnp.sqrt(v + eps)

def _scatter_add(tgt, idx, src, axis=0):
    return tgt.at[idx].add(src)

def _segment_sum(src, seg, n):
    return jax.ops.segment_sum(src, seg, n)
kernel_name = 'mk_gnn_ffn_d1_gnn_r32_2652e0'

def setup_inputs(seed: int=0):
    np.random.seed(seed)
    _w = jnp.asarray

    def _rec_inputs():
        import jax
        import jax.numpy as jnp
        _gk = jax.random.key(seed)
        x = -0.0003713 + 1 * jax.random.normal(jax.random.fold_in(_gk, 1), (50000, 256), jnp.float32)
        src = jax.random.randint(jax.random.fold_in(_gk, 2), (50000,), 0, 50000, jnp.int32)
        dst = jax.random.randint(jax.random.fold_in(_gk, 3), (50000,), 0, 50000, jnp.int32)
        _o = jnp.argsort(dst, stable=True)
        src = src[_o]
        dst = dst[_o]
        return (x, src, dst)
    x, src, dst = _rec_inputs()

    def _L0_gnn_setup():
        import jax, jax.numpy as jnp
        import numpy as np
        N, E, D_IN, D_OUT = (50000, 50000, 256, 256)
        key = jax.random.key(seed)
        k1, k2, k3, k4, k5, k6 = jax.random.split(key, 6)
        x = jax.random.normal(k1, (N, D_IN), dtype=jnp.float32)
        edge_index = jax.random.randint(k2, (2, E), 0, N, dtype=jnp.int64)
        s = 1.0 / np.sqrt(D_IN)
        W1 = jax.random.uniform(k3, (D_OUT, D_IN), minval=-s, maxval=s, dtype=jnp.float32)
        b1 = jax.random.uniform(k4, (D_OUT,), minval=-s, maxval=s, dtype=jnp.float32)
        W2 = jax.random.uniform(k5, (D_OUT, D_IN), minval=-s, maxval=s, dtype=jnp.float32)
        b2 = jax.random.uniform(k6, (D_OUT,), minval=-s, maxval=s, dtype=jnp.float32)
        return {'x': x, 'W1': W1, 'b1': b1, 'W2': W2, 'b2': b2, 'edge_index': edge_index}
    _L0_gnn_all = _L0_gnn_setup()
    _L0_gnn_in = {k: v for k, v in _L0_gnn_all.items() if k in ('W1', 'b1', 'W2', 'b2')}
    del _L0_gnn_all

    def _L0_ffn_setup():
        import jax, jax.numpy as jnp
        import numpy as np
        B, A = (128, 8)
        IN, OUT = (256, 256)
        SH1, SH2 = (256, 128)
        EH1, EH2 = (128, 64)
        E, TOPK = (4, 2)

        def _shared_mlp(x, W1, b1, W2, b2, W3, b3):
            h = jax.nn.relu(x @ W1 + b1)
            h = jax.nn.relu(h @ W2 + b2)
            return h @ W3 + b3

        def _experts_mlp(x, eW1, eb1, eW2, eb2, eW3, eb3):
            h = jax.nn.relu(jnp.einsum('baf,efh->ebah', x, eW1) + eb1[:, None, None, :])
            h = jax.nn.relu(jnp.einsum('ebah,ehg->ebag', h, eW2) + eb2[:, None, None, :])
            o = jnp.einsum('ebag,ego->ebao', h, eW3) + eb3[:, None, None, :]
            return jnp.moveaxis(o, 0, -1)
        key = jax.random.key(seed)
        ks = jax.random.split(key, 16)
        s = 0.05
        return {'x': jax.random.normal(ks[0], (B, A, IN), jnp.float32), 'sW1': jax.random.normal(ks[1], (IN, SH1), jnp.float32) * s, 'sb1': jnp.zeros((SH1,), jnp.float32), 'sW2': jax.random.normal(ks[2], (SH1, SH2), jnp.float32) * s, 'sb2': jnp.zeros((SH2,), jnp.float32), 'sW3': jax.random.normal(ks[3], (SH2, OUT), jnp.float32) * s, 'sb3': jnp.zeros((OUT,), jnp.float32), 'eW1': jax.random.normal(ks[4], (E, IN, EH1), jnp.float32) * s, 'eb1': jnp.zeros((E, EH1), jnp.float32), 'eW2': jax.random.normal(ks[5], (E, EH1, EH2), jnp.float32) * s, 'eb2': jnp.zeros((E, EH2), jnp.float32), 'eW3': jax.random.normal(ks[6], (E, EH2, OUT), jnp.float32) * s, 'eb3': jnp.zeros((E, OUT), jnp.float32), 'gW': jax.random.normal(ks[7], (IN, E), jnp.float32) * s, 'gb': jnp.zeros((E,), jnp.float32)}
    _L0_ffn_all = _L0_ffn_setup()
    _L0_ffn_in = {k: v for k, v in _L0_ffn_all.items() if k in ('sW1', 'sb1', 'sW2', 'sb2', 'sW3', 'sb3', 'eW1', 'eb1', 'eW2', 'eb2', 'eW3', 'eb3', 'gW', 'gb')}
    del _L0_ffn_all
    return {'x': x, 'src': src, 'dst': dst, 'L0_gnn_W1': _L0_gnn_in['W1'], 'L0_gnn_b1': _L0_gnn_in['b1'], 'L0_gnn_W2': _L0_gnn_in['W2'], 'L0_gnn_b2': _L0_gnn_in['b2'], 'L0_ffn_sW1': _L0_ffn_in['sW1'], 'L0_ffn_sb1': _L0_ffn_in['sb1'], 'L0_ffn_sW2': _L0_ffn_in['sW2'], 'L0_ffn_sb2': _L0_ffn_in['sb2'], 'L0_ffn_sW3': _L0_ffn_in['sW3'], 'L0_ffn_sb3': _L0_ffn_in['sb3'], 'L0_ffn_eW1': _L0_ffn_in['eW1'], 'L0_ffn_eb1': _L0_ffn_in['eb1'], 'L0_ffn_eW2': _L0_ffn_in['eW2'], 'L0_ffn_eb2': _L0_ffn_in['eb2'], 'L0_ffn_eW3': _L0_ffn_in['eW3'], 'L0_ffn_eb3': _L0_ffn_in['eb3'], 'L0_ffn_gW': _L0_ffn_in['gW'], 'L0_ffn_gb': _L0_ffn_in['gb']}

def reference(x, src, dst, L0_gnn_W1, L0_gnn_b1, L0_gnn_W2, L0_gnn_b2, L0_ffn_sW1, L0_ffn_sb1, L0_ffn_sW2, L0_ffn_sb2, L0_ffn_sW3, L0_ffn_sb3, L0_ffn_eW1, L0_ffn_eb1, L0_ffn_eW2, L0_ffn_eb2, L0_ffn_eW3, L0_ffn_eb3, L0_ffn_gW, L0_ffn_gb):
    import jax
    import jax.numpy as jnp

    def _L0_gnn_ref(x, W1, b1, W2, b2, edge_index):
        import jax, jax.numpy as jnp
        import numpy as np
        N, E, D_IN, D_OUT = (50000, 50000, 256, 256)
        dst = edge_index[0]
        nbr = edge_index[1]
        n = x.shape[0]
        agg = jax.ops.segment_sum(x[nbr], dst, num_segments=n)
        cnt = jax.ops.segment_sum(jnp.ones((nbr.shape[0],), x.dtype), dst, num_segments=n)
        mean = agg / jnp.maximum(cnt, 1.0)[:, None]
        return x @ W1.T + b1 + mean @ W2.T + b2

    def _L0_ffn_ref(x, sW1, sb1, sW2, sb2, sW3, sb3, eW1, eb1, eW2, eb2, eW3, eb3, gW, gb):
        import jax, jax.numpy as jnp
        import numpy as np
        B, A = (128, 8)
        IN, OUT = (256, 256)
        SH1, SH2 = (256, 128)
        EH1, EH2 = (128, 64)
        E, TOPK = (4, 2)

        def _shared_mlp(x, W1, b1, W2, b2, W3, b3):
            h = jax.nn.relu(x @ W1 + b1)
            h = jax.nn.relu(h @ W2 + b2)
            return h @ W3 + b3

        def _experts_mlp(x, eW1, eb1, eW2, eb2, eW3, eb3):
            h = jax.nn.relu(jnp.einsum('baf,efh->ebah', x, eW1) + eb1[:, None, None, :])
            h = jax.nn.relu(jnp.einsum('ebah,ehg->ebag', h, eW2) + eb2[:, None, None, :])
            o = jnp.einsum('ebag,ego->ebao', h, eW3) + eb3[:, None, None, :]
            return jnp.moveaxis(o, 0, -1)
        all_out = _experts_mlp(x, eW1, eb1, eW2, eb2, eW3, eb3)
        shared = _shared_mlp(x, sW1, sb1, sW2, sb2, sW3, sb3)
        gates = jax.nn.softmax(x @ gW + gb, axis=-1)
        topv, topi = jax.lax.top_k(gates, TOPK)
        topw = jax.nn.softmax(topv, axis=-1)
        sel = jnp.take_along_axis(all_out, topi[:, :, None, :], axis=-1)
        gated = jnp.sum(sel * topw[:, :, None, :], axis=-1)
        return shared + gated
    edge_index = jnp.stack([src, dst])
    x = x + _L0_gnn_ref(_layernorm(x, axis=-1), L0_gnn_W1, L0_gnn_b1, L0_gnn_W2, L0_gnn_b2, edge_index)
    x = x + _L0_ffn_ref(_layernorm(x, axis=-1)[None], L0_ffn_sW1, L0_ffn_sb1, L0_ffn_sW2, L0_ffn_sb2, L0_ffn_sW3, L0_ffn_sb3, L0_ffn_eW1, L0_ffn_eb1, L0_ffn_eW2, L0_ffn_eb2, L0_ffn_eW3, L0_ffn_eb3, L0_ffn_gW, L0_ffn_gb)[0]
    return x

_drawn_inputs = setup_inputs


def setup_inputs(seed=0):
    import zlib

    import numpy as np

    out = dict(_drawn_inputs(seed))
    spreads = {'L0_ffn_sb1': (0.0, 0.491),
     'L0_ffn_sb2': (0.0, 0.1),
     'L0_ffn_sb3': (0.0, 0.1),
     'L0_ffn_eb1': (0.0, 0.8),
     'L0_ffn_eb2': (0.0, 0.585),
     'L0_ffn_eb3': (0.0, 0.1),
     'L0_ffn_gb': (0.0, 0.431)}
    factors = {}
    for name, (base, spread) in spreads.items():
        noise = np.random.default_rng([zlib.crc32(name.encode()), seed]).standard_normal(out[name].shape)
        drawn = base * np.exp(spread * noise) if base else spread * noise
        out[name] = jnp.asarray(drawn.astype(out[name].dtype))
    for name, factor in factors.items():
        out[name] = (out[name] * factor).astype(out[name].dtype)
    return out
```

```python
from contextlib import ExitStack

import numpy as np

import concourse.bass as bass
from concourse import mybir

F32, F32R, F16, I32 = mybir.dt.float32, mybir.dt.float32r, mybir.dt.float16, mybir.dt.int32
ALU = mybir.AluOpType
ACT = mybir.ActivationFunctionType
AX = mybir.AxisListType

P = 128
N = 50000
E = 50000
D = 256
FT = D // P
GN = 500
NG = N // GN
SP_ = 125
NS = GN // SP_
EQ = 5
CAP = EQ * P
NT = NG * EQ
EP = 125
EC = E // EP
CB = 5
UNR = 4
NX = 4
H1T = 6
H2T = 3
NB3 = 14
NF1 = 4
L1_BANKS = (0, 1, 4, 5, 0, 1)
EPS = 1e-5
RND = 12582912.0


def build(nc, x, src, dst, w1t, w2t, b12, wl1, bl1, wl2, bl2, wl3, b3, gw, gb,
          ident, ident16, upper16, iota16, iota, selg, tie, out, agg_x, cnt_x):
    with ExitStack() as ctx:
        def sem(name):
            return ctx.enter_context(nc.semaphore(name))

        def sb(name, shape, dt, c=ctx):
            return c.enter_context(nc.sbuf_tensor(name, shape, dt))

        bank = [ctx.enter_context(nc.psum_tensor(f"bank{b}", [P, 512], F32)) for b in range(8)]

        ident_sb = sb("ident_sb", [P, P], F32)
        iota_sb = sb("iota_sb", [P, GN], F32)
        bias12 = sb("bias12", [P, NS, D], F32)
        bl1_sb = sb("bl1_sb", [P, H1T], F32)
        bl2_sb = sb("bl2_sb", [P, H2T], F32)
        gb_sb = sb("gb_sb", [P, NX], F32)
        tie_sb = sb("tie_sb", [P, NX, NX], F32)
        half_neg = sb("half_neg", [P, EQ], F32)
        ones_r = sb("ones_r", [P, 8], F32R)
        zeros_r = sb("zeros_r", [P, 8], F32R)
        w1_hl = sb("w1_hl", [P, 2, FT, D], F32R)
        w2_hl = sb("w2_hl", [P, 2, FT, D], F32R)
        wl1_hl = sb("wl1_hl", [P, 2, FT, H1T * P], F32R)
        wl2_hl = sb("wl2_hl", [P, 2, 6, P], F32R)
        wl3_hl = sb("wl3_hl", [P, 2, H2T, D], F32R)
        gw_hl = sb("gw_hl", [P, 2, FT, 8], F32R)
        b3_r = sb("b3_r", [NB3, D], F32R)
        selg_r = sb("selg_r", [NB3, 2, P], F32R)
        src_of_slot = sb("src_of_slot", [P, NT], I32)
        col_of_slot = sb("col_of_slot", [P, NT], F32)
        rounds_sb = sb("rounds_sb", [1, 1], I32)

        s_passed = sem("lone_waits_passed")
        def wait_alone(eng, on, value):
            eng.wait_ge(on, value)
            if not isinstance(value, int):
                eng.sem_inc(s_passed, 1)

        s_w = sem("weights_loaded")
        s_cst = sem("constants_loaded")
        s_edge_in = sem("edges_loaded")
        s_bs = sem("bias_ready")

        with ExitStack() as c0:
            stage = {}
            parts = (("w1", w1t, w1_hl, 1), ("w2", w2t, w2_hl, 1), ("wl1", wl1, wl1_hl, 1),
                     ("wl2", wl2, wl2_hl, 1), ("wl3", wl3, wl3_hl, 1))
            for nm, ap, hl, _ in parts:
                stage[nm] = sb("st_" + nm, [P, *hl.shape[2:]], F32, c0)
            st_gw = sb("st_gw", [P, FT, NX], F32, c0)
            st_b3 = sb("st_b3", [NB3, D], F32, c0)
            st_b3b = sb("st_b3b", [NB3, D], F32, c0)
            st_sel = sb("st_sel", [NB3, 3, P], F32, c0)
            st_b = sb("st_b", [P, 2, D], F32, c0)
            b3_hi = sb("b3_hi", [NB3, D], F32R, c0)
            b3_lo = sb("b3_lo", [NB3, D], F32, c0)
            s_hi = sem("weight_high_ready")
            s_lo = sem("weight_low_ready")

            with nc.Block() as block:
                @block.sync
                def _(sp):
                    for nm, ap, _, _ in parts:
                        sp.dma_start(stage[nm][:], ap).then_inc(s_w, 16)
                    sp.dma_start(st_gw[:], gw).then_inc(s_w, 16)
                    sp.dma_start(st_b3[:], b3).then_inc(s_w, 16)
                    sp.dma_start(st_sel[:], selg).then_inc(s_w, 16)
                    sp.dma_start(st_b[:], b12.partition_broadcast(P)).then_inc(s_w, 16)
                    sp.dma_start(ident_sb[:], ident).then_inc(s_cst, 16)
                    sp.dma_start(iota_sb[:], iota).then_inc(s_cst, 16)
                    sp.dma_start(bl1_sb[:], bl1).then_inc(s_cst, 16)
                    sp.dma_start(bl2_sb[:], bl2).then_inc(s_cst, 16)
                    sp.dma_start(gb_sb[:], gb.partition_broadcast(P)).then_inc(s_cst, 16)
                    sp.dma_start(tie_sb[:], tie).then_inc(s_cst, 16)

                @block.vector
                def _(dve):
                    dve.wait_ge(s_w, 16 * 9)
                    n = 0
                    for nm, _, hl, _ in parts:
                        dve.tensor_copy(hl[:, 0], stage[nm][:]).then_inc(s_hi, 1)
                        n += 1
                        dve.wait_ge(s_hi, n)
                        dve.tensor_tensor(hl[:, 1], stage[nm][:], hl[:, 0].bitcast(F32),
                                          ALU.subtract).then_inc(s_lo, 1)
                    dve.tensor_copy(gw_hl[:, 0, :, 0:NX], st_gw[:]).then_inc(s_hi, 1)
                    dve.tensor_copy(gw_hl[:, 1, :, 0:NX], st_gw[:]).then_inc(s_hi, 1)
                    dve.memset(gw_hl[:, 1, :, NX:8].bitcast(F32), 0.0).then_inc(s_lo, 1)
                    dve.wait_ge(s_hi, n + 2)
                    dve.tensor_tensor(gw_hl[:, 0, :, NX:8], st_gw[:],
                                      gw_hl[:, 0, :, 0:NX].bitcast(F32),
                                      ALU.subtract).then_inc(s_lo, 1)
                    dve.tensor_copy(b3_hi[:], st_b3[:]).then_inc(s_hi, 1)
                    dve.wait_ge(s_hi, n + 3)
                    dve.tensor_tensor(b3_lo[:], st_b3[:], b3_hi[:].bitcast(F32),
                                      ALU.subtract).then_inc(s_hi, 1)
                    dve.wait_ge(s_hi, n + 4)
                    dve.tensor_scalar(st_b3b[:], b3_lo[:], st_sel[:, 2, 1:2], None,
                                      ALU.mult).then_inc(s_hi, 1)
                    dve.wait_ge(s_hi, n + 5)
                    dve.scalar_tensor_tensor(out=b3_r[:], in0=b3_hi[:].bitcast(F32),
                                             scalar=st_sel[:, 2, 0:1], in1=st_b3b[:],
                                             op0=ALU.mult, op1=ALU.add).then_inc(s_lo, 1)
                    dve.tensor_copy(selg_r[:], st_sel[:, 0:2]).then_inc(s_lo, 1)
                    for s in range(NS):
                        dve.tensor_tensor(bias12[:, s], st_b[:, 0], st_b[:, 1],
                                          ALU.add).then_inc(s_bs, 1)
                    dve.memset(half_neg[:], -0.5).then_inc(s_bs, 1)
                    dve.memset(ones_r[:].bitcast(F32), 1.0).then_inc(s_bs, 1)
                    dve.memset(zeros_r[:].bitcast(F32), 0.0).then_inc(s_bs, 1)

        with ExitStack() as c1:
            id16 = sb("id16", [NG, 2, NG], F16, c1)
            up16 = sb("up16", [EP, EP], F16, c1)
            io16 = sb("io16", [P, GN], F16, c1)
            ones16 = sb("ones16", [EP, 2], F16, c1)
            zero16 = sb("zero16", [EP, GN], F16, c1)
            ones_scan = sb("ones_scan", [NG, EC], F32, c1)
            ei = sb("ei", [EP, 2, EC], I32, c1)
            ef = sb("ef", [EP, 2, EC], F32, c1)
            t0 = sb("t0", [EP, EC], F32, c1)
            t1 = sb("t1", [EP, EC], F32, c1)
            t2 = sb("t2", [EP, EC], F32, c1)
            grp = sb("grp", [EP, EC], F32, c1)
            grp16 = sb("grp16", [EP, EC], F16, c1)
            val16 = sb("val16", [EP, 3, EC], F16, c1)
            rank = sb("rank", [EP, EC], F32, c1)
            slot16 = sb("slot16", [EP, EC], F16, c1)
            tcol = sb("tcol", [EP, EC], F32, c1)
            before = sb("before", [NG, EC], F32, c1)
            bef16 = sb("bef16", [NG, 2, EC], F16, c1)
            rows1 = sb("slot_oh", [EP, 2, CB, P], F16, c1)
            rowsv = sb("slot_val", [EP, 2, 3, CB, P], F16, c1)
            cols1 = sb("cols1", [EP, 2, CB, NT], F16, c1)
            tmax = sb("tmax", [1, 4], F32, c1)
            tsum = sb("tsum", [P, NT], F32, c1)
            rank_r = sb("rank_r", [EP, EC], F32, c1)
            c_oh = ExitStack()
            oh = sb("oh", [EP, EC, NG], F16, c_oh)
            prod = sb("prod", [EP, 2, CB, NG], F32, c_oh)

            s_c = sem("sort_step")
            s_c0 = sem("sort_constants_loaded")
            s_oh = sem("group_onehots_ready")
            s_tot = sem("chunk_counts_ready")
            s_bef = sem("prefix_parts_ready")
            s_pre = sem("prefix_in_psum")
            s_prod = sem("prefix_selected")
            s_rank = sem("ranks_ready")
            s_max = sem("largest_group_row")
            s_rnd = sem("round_count_ready")

            NIT = EC // (CB * UNR)

            def dve_steps(dve):
                count = [0]

                def step(ins):
                    ins.then_inc(s_c, 1)
                    count[0] += 1
                    dve.wait_ge(s_c, count[0])
                return step

            with nc.Block() as block:
                @block.sync
                def _(sp):
                    sp.dma_start(ei[:, 0], src).then_inc(s_edge_in, 16)
                    sp.dma_start(ei[:, 1], dst).then_inc(s_edge_in, 16)
                    sp.dma_start(io16[:], iota16).then_inc(s_c0, 16)
                    sp.dma_start(up16[:], upper16).then_inc(s_c0, 16)
                    sp.dma_start(id16[:], ident16).then_inc(s_c0, 16)

                @block.vector
                def _(dve):
                    step = dve_steps(dve)
                    dve.memset(ones_scan[:], 1.0).then_inc(s_bef, 1)
                    dve.memset(zero16[:], 0.0).then_inc(s_bef, 1)
                    dve.memset(ones16[:], 1.0).then_inc(s_bef, 1)
                    dve.wait_ge(s_edge_in, 32)
                    step(dve.tensor_copy(ef[:], ei[:]))
                    step(dve.tensor_scalar(t0[:], ef[:, 0], 1.0 / GN, -0.499, ALU.mult, ALU.add))
                    step(dve.tensor_scalar(grp[:], t0[:], RND, RND, ALU.add, ALU.subtract))
                    step(dve.tensor_copy(grp16[:], grp[:]))
                    dve.wait_ge(s_c0, 48)
                    for k in range(10):
                        a = slice(k * EC // 10, (k + 1) * EC // 10)
                        w = EC // 10
                        dve.tensor_tensor(
                            oh[:, a], grp16[:, a].unsqueeze(2).to_broadcast([EP, w, NG]),
                            io16[0:EP, 0:NG].unsqueeze(1).to_broadcast([EP, w, NG]),
                            ALU.is_equal).then_inc(s_oh, 1)
                    step(dve.scalar_tensor_tensor(out=t1[:], in0=grp[:], scalar=-float(GN),
                                                  in1=ef[:, 0], op0=ALU.mult, op1=ALU.add))
                    step(dve.tensor_scalar(t0[:], t1[:], 1.0 / NS, -0.375, ALU.mult, ALU.add))
                    step(dve.tensor_scalar(t2[:], t0[:], RND, RND, ALU.add, ALU.subtract))
                    step(dve.scalar_tensor_tensor(out=t0[:], in0=t2[:], scalar=-float(NS),
                                                  in1=t1[:], op0=ALU.mult, op1=ALU.add))
                    step(dve.tensor_scalar(t1[:], t0[:], float(SP_), 1.0, ALU.mult, ALU.add))
                    step(dve.tensor_tensor(val16[:, 2], t1[:], t2[:], ALU.add))
                    step(dve.tensor_scalar(t1[:], ef[:, 1], 1.0, None, ALU.add))
                    step(dve.tensor_scalar(t0[:], t1[:], 1.0 / 256, -0.498, ALU.mult, ALU.add))
                    step(dve.tensor_scalar(t2[:], t0[:], RND, RND, ALU.add, ALU.subtract))
                    step(dve.tensor_copy(val16[:, 0], t2[:]))
                    step(dve.scalar_tensor_tensor(out=val16[:, 1], in0=t2[:], scalar=-256.0,
                                                  in1=t1[:], op0=ALU.mult, op1=ALU.add))
                    dve.wait_ge(s_tot, NIT)
                    dve.wait_ge(s_bef, 3)
                    step(dve.tensor_tensor_scan(before[:], ones_scan[:], bank[0][0:NG, 0:EC], 0.0,
                                                ALU.mult, ALU.add))
                    dve.tensor_copy(ones_scan[:, 0:1], before[:, EC - 1:EC]).then_inc(s_max, 1)
                    dve.wait_ge(s_max, 1)
                    step(dve.tensor_tensor(before[:], before[:], bank[0][0:NG, 0:EC],
                                           ALU.subtract))
                    step(dve.tensor_scalar(ones_scan[:, 1:EC], before[:, 1:EC], 1.0 / 256, -0.498,
                                           ALU.mult, ALU.add))
                    step(dve.tensor_scalar(bef16[:, 0, 1:EC], ones_scan[:, 1:EC], RND, RND,
                                           ALU.add, ALU.subtract))
                    step(dve.memset(bef16[:, 0, 0:1], 0.0))
                    step(dve.scalar_tensor_tensor(out=bef16[:, 1], in0=bef16[:, 0], scalar=-256.0,
                                                  in1=before[:], op0=ALU.mult, op1=ALU.add))
                    dve.nop().then_inc(s_bef, 1)
                    dve.nop().then_inc(s_prod, 2)
                    with dve.Fori(0, NIT) as it:
                        for u in range(UNR):
                            h = u % 2
                            dve.wait_ge(s_pre, it * UNR + (u + 1))
                            c0_ = it * (UNR * CB) + u * CB
                            dve.tensor_tensor(
                                prod[:, h],
                                bank[1 + h][0:EP, 0:CB * NG].rearrange("p (c g) -> p c g", c=CB),
                                oh[:, bass.ds(c0_, CB)], ALU.mult).then_inc(s_prod, 1)
                            dve.wait_ge(s_prod, it * UNR + (u + 3))
                            dve.tensor_reduce(rank[:, bass.ds(c0_, CB)], prod[:, h], AX.X,
                                              ALU.add).then_inc(s_rank, 1)
                    dve.wait_ge(s_max, 2)
                    step(dve.tensor_reduce(tmax[:, 0:1], bank[3][0:1, 0:NG], AX.X, ALU.max))
                    step(dve.tensor_scalar(tmax[:, 1:2], tmax[:, 0:1], 1.0 / CAP, 0.4995,
                                           ALU.mult, ALU.add))
                    step(dve.tensor_scalar(tmax[:, 2:3], tmax[:, 1:2], RND, RND, ALU.add,
                                           ALU.subtract))
                    step(dve.tensor_copy(rounds_sb[:], tmax[:, 2:3]))

                @block.tensor
                def _(pe):
                    with pe.Fori(0, NIT) as it:
                        for u in range(UNR * CB):
                            if u == 0:
                                pe.wait_ge(s_oh, 10)
                                pe.wait_ge(s_bef, 3)
                            c = it * (UNR * CB) + u
                            mm = pe.matmul(bank[0][0:NG, bass.ds(c, 1)], oh[:, c, :],
                                           ones16[:, 0:1], start=True, stop=True)
                        mm.then_inc(s_tot, 1)
                    pe.wait_ge(s_bef, 4)
                    with pe.Fori(0, NIT) as it:
                        for u in range(UNR):
                            h = u % 2
                            pe.wait_ge(s_prod, it * UNR + (u + 1))
                            for j in range(CB):
                                c = it * (UNR * CB) + (u * CB + j)
                                o = bank[1 + h][0:EP, j * NG:(j + 1) * NG]
                                pe.matmul(o, up16[:], oh[:, c, :], start=True, stop=False)
                                for part in range(2):
                                    mm = pe.matmul(
                                        o, bef16[:, part, bass.ds(c, 1)].to_broadcast([NG, EP]),
                                        id16[:, 1 - part, :], start=False, stop=part == 1)
                            mm.then_inc(s_pre, 1)
                    pe.wait_ge(s_max, 1)
                    pe.transpose(bank[3][0:1, 0:NG], ones_scan[:, 0:1],
                                 ident_sb[0:NG, 0:NG]).then_inc(s_max, 1)


            c_oh.close()

            class TableSems:
                def __init__(self, tag, ahead):
                    self.ahead = ahead
                    self.step = sem(tag + "table_step")
                    self.row1 = sem(tag + "slot_onehots_ready")
                    self.rowv = sem(tag + "slot_values_ready")
                    self.rowc = sem(tag + "slot_columns_ready")
                    self.col = sem(tag + "table_onehots_ready")
                    self.added = sem(tag + "table_chunks_added")
                    self.sums = sem(tag + "table_sums_done")
                    self.out = sem(tag + "table_written")

            NB = NIT * UNR

            def table_vector(dve, T, r, rk):
                steps = [0]

                def step(ins):
                    ins.then_inc(T.step, 1)
                    steps[0] += 1
                    if steps[0] < 7:
                        dve.wait_ge(T.step, r * 7 + steps[0])
                    else:
                        wait_alone(dve, T.step, r * 7 + 7)
                step(dve.tensor_scalar(t0[:], rk[:], 1.0 / P, -0.498, ALU.mult, ALU.add))
                step(dve.tensor_scalar(t1[:], t0[:], RND, RND, ALU.add, ALU.subtract))
                step(dve.scalar_tensor_tensor(out=t0[:], in0=t1[:], scalar=-float(P),
                                              in1=rk[:], op0=ALU.mult, op1=ALU.add))
                step(dve.tensor_scalar(t2[:], t1[:], 0.0, None, ALU.is_lt))
                step(dve.scalar_tensor_tensor(out=tcol[:], in0=t1[:], scalar=EQ - 0.5, in1=t2[:],
                                              op0=ALU.is_gt, op1=ALU.add))
                step(dve.scalar_tensor_tensor(out=slot16[:], in0=tcol[:], scalar=1000.0,
                                              in1=t0[:], op0=ALU.mult, op1=ALU.add))
                step(dve.scalar_tensor_tensor(out=tcol[:], in0=grp[:], scalar=float(EQ),
                                              in1=t1[:], op0=ALU.mult, op1=ALU.add))
                with dve.Fori(0, NIT) as it:
                    for u in range(UNR):
                        h = u % 2
                        at = it * (UNR * CB) + u * CB
                        n = r * NB + it * UNR + u
                        dve.wait_ge(T.added, r * (NB + 2) + it * UNR + (u + 1))
                        dve.tensor_tensor(
                            rows1[:, h],
                            slot16[:, bass.ds(at, CB)].unsqueeze(2).to_broadcast([EP, CB, P]),
                            io16[0:EP, 0:P].unsqueeze(1).to_broadcast([EP, CB, P]),
                            ALU.is_equal).then_inc(T.row1, 1)
                        for j in range(CB):
                            ins = dve.tensor_scalar(cols1[:, h, j], io16[0:EP, 0:NT],
                                                    tcol[:, bass.ds(at + j, 1)], None,
                                                    ALU.is_equal)
                        ins.then_inc(T.col, 1)
                        dve.wait_ge(T.row1, n + 1)
                        for v in range(2):
                            ins = dve.tensor_tensor(
                                rowsv[:, h, v], rows1[:, h],
                                val16[:, v, bass.ds(at, CB)].unsqueeze(2)
                                .to_broadcast([EP, CB, P]), ALU.mult)
                        ins.then_inc(T.rowv, 1)
                dve.wait_ge(T.sums, r + 1)
                dve.tensor_scalar(tsum[:], bank[0][:, 0:NT], 256.0, -1.0, ALU.mult,
                                  ALU.add).then_inc(T.out, 1)
                dve.tensor_copy(col_of_slot[:], bank[2][:, 0:NT]).then_inc(T.out, 1)
                dve.wait_ge(T.out, r * 3 + (2 + T.ahead))
                dve.tensor_tensor(src_of_slot[:], tsum[:], bank[1][:, 0:NT],
                                  ALU.add).then_inc(T.out, 1)

            def table_pool(pool, T, r):
                with pool.Fori(0, NIT) as it:
                    for u in range(UNR):
                        h = u % 2
                        at = it * (UNR * CB) + u * CB
                        pool.wait_ge(T.row1, r * NB + it * UNR + (u + 1))
                        pool.tensor_tensor(
                            rowsv[:, h, 2], rows1[:, h],
                            val16[:, 2, bass.ds(at, CB)].unsqueeze(2)
                            .to_broadcast([EP, CB, P]), ALU.mult).then_inc(T.rowc, 1)

            def table_tensor(pe, T, r):
                if not isinstance(r, int):
                    pe.wait_ge(T.out, r * 3 + T.ahead)
                for v in range(3):
                    mm = pe.matmul(bank[v][:, 0:NT], zero16[:, 0:P], zero16[:, 0:NT],
                                   start=True, stop=False)
                    if v:
                        mm.then_inc(T.added, 1)
                with pe.Fori(0, NIT) as it:
                    for u in range(UNR):
                        h = u % 2
                        n = r * NB + it * UNR + (u + 1)
                        pe.wait_ge(T.col, n)
                        pe.wait_ge(T.rowv, n)
                        pe.wait_ge(T.rowc, n)
                        for v in range(3):
                            for j in range(CB):
                                mm = pe.matmul(bank[v][:, 0:NT], rowsv[:, h, v, j],
                                               cols1[:, h, j], start=False, stop=False)
                        mm.then_inc(T.added, 1)
                for v in range(3):
                    mm = pe.matmul(bank[v][:, 0:NT], zero16[:, 0:P], zero16[:, 0:NT],
                                   start=False, stop=True)
                mm.then_inc(T.sums, 1)

            with ExitStack() as cx:
                r_slots = sb("r_slots", [P, EQ], I32, cx)
                r_rows = sb("r_rows", [P, EQ, D], F32, cx)
                r_hi = sb("r_hi", [P, EQ, D], F32R, cx)
                r_lo = sb("r_lo", [P, EQ, D], F32R, cx)
                r_oh = sb("r_oh", [P, EQ, GN], F32R, cx)
                r_st = sb("r_st", [P, EQ, 6], F32, cx)
                r_mv = sb("r_mv", [P, EQ, 2], F32, cx)
                r_var = sb("r_var", [P, EQ], F32, cx)
                r_rstd = sb("r_rstd", [P, EQ], F32, cx)
                r_sum = sb("r_sum", [P, FT, GN], F32, cx)
                r_cnt = sb("r_cnt", [8, GN], F32, cx)
                VS = 4 * EQ + 2 + FT
                TX = TableSems("more_", 1)
                R = {n: sem("more_" + n) for n in
                     "zeros cleared slots gathered stats rstd vector split sums out added".split()}

                with nc.Block() as block:
                    @block.sync
                    def _(sp):
                        rounds = sp.value_load(rounds_sb[0:1, 0:1], min_val=1, max_val=E // CAP + 1)
                        with sp.If(rounds > 1):
                            sp.wait_ge(R["zeros"], 2)
                            with sp.Fori(0, NG) as g:
                                sp.dma_start(agg_x[bass.ds(g, 1)][0],
                                             r_sum[:].rearrange("p f n -> p (f n)"))\
                                  .then_inc(R["cleared"], 16)
                                sp.dma_start(cnt_x[bass.ds(g, 1)][0], r_cnt[:])\
                                  .then_inc(R["cleared"], 16)
                            sp.wait_ge(R["cleared"], 32 * NG)

                    @block.gpsimd
                    def _(pool):
                        rounds = pool.value_load(rounds_sb[0:1, 0:1], min_val=1,
                                                 max_val=E // CAP + 1)
                        with pool.If(rounds > 1):
                            pool.wait_ge(R["cleared"], 32 * NG)
                            with pool.Fori(0, rounds - 1) as r:
                                table_pool(pool, TX, r)
                                wait_alone(pool, TX.out, r * 3 + 4)
                                with pool.Fori(0, NG) as g:
                                    n = r * NG + g
                                    pool.tensor_copy(r_slots[:],
                                                     src_of_slot[:, bass.ds(g * EQ, EQ)])\
                                        .then_inc(R["slots"], 1)
                                    wait_alone(pool, R["slots"], n + 1)
                                    for q in range(EQ):
                                        pool.indirect_dma_start(
                                            out=r_rows[:, q, :], out_offset=None, in_=x,
                                            in_offset=bass.IndirectOffsetOnAxis(
                                                ap=r_slots[:, q:q + 1], axis=0),
                                            bounds_check=N - 1,
                                            oob_is_err=False).then_inc(R["gathered"], 16)
                                    wait_alone(pool, R["stats"], n + 1)
                                    pool.tensor_scalar(r_var[:], r_mv[:, :, 1], EPS, None,
                                                       ALU.add).then_inc(R["rstd"], 1)
                                    pool.wait_ge(R["rstd"], n * 2 + 1)
                                    pool.tensor_tensor(r_rstd[:], r_var[:], half_neg[:],
                                                       ALU.pow).then_inc(R["rstd"], 1)
                                    pool.wait_ge(R["out"], n + 1)
                                    pool.dma_start(agg_x[bass.ds(g, 1)][0],
                                                   r_sum[:].rearrange("p f n -> p (f n)"),
                                                   accum_op=ALU.add).then_inc(R["added"], 16)
                                    pool.dma_start(cnt_x[bass.ds(g, 1)][0], r_cnt[:],
                                                   accum_op=ALU.add).then_inc(R["added"], 16)
                                    wait_alone(pool, R["added"], n * 32 + 32)

                    @block.vector
                    def _(dve):
                        rounds = dve.value_load(rounds_sb[0:1, 0:1], min_val=1,
                                                max_val=E // CAP + 1)
                        with dve.If(rounds > 1):
                            dve.memset(r_sum[:], 0.0).then_inc(R["zeros"], 1)
                            dve.memset(r_cnt[:], 0.0).then_inc(R["zeros"], 1)
                            dve.memset(r_rows[:], 0.0).then_inc(R["split"], 1)
                            dve.tensor_copy(rank_r[:], rank[:]).then_inc(R["split"], 1)
                            dve.nop().then_inc(TX.out, 1)
                            dve.wait_ge(R["split"], 2)
                            with dve.Fori(0, rounds - 1) as r:
                                dve.tensor_scalar(rank_r[:], rank_r[:], -float(CAP), None,
                                                  ALU.add).then_inc(R["split"], 1)
                                dve.wait_ge(R["split"], r * (NG + 1) + 3)
                                table_vector(dve, TX, r, rank_r)
                                with dve.Fori(0, NG) as g:
                                    n = r * NG + g
                                    steps = [0]

                                    def step(ins, k=1):
                                        ins.then_inc(R["vector"], 1)
                                        steps[0] += 1
                                        if k:
                                            dve.wait_ge(R["vector"], n * VS + steps[0])
                                    dve.wait_ge(R["gathered"], n * (16 * EQ) + 16 * EQ)
                                    for q in range(EQ):
                                        step(dve.bn_stats(r_st[:, q, :], r_rows[:, q, :]), 0)
                                    wait_alone(dve, R["vector"], n * VS + EQ)
                                    for q in range(EQ):
                                        step(dve.bn_aggr(r_mv[:, q, :], r_st[:, q, :]), 0)
                                    dve.wait_ge(R["vector"], n * VS + 2 * EQ)
                                    dve.nop().then_inc(R["stats"], 1)
                                    dve.wait_ge(R["rstd"], n * 2 + 2)
                                    for q in range(EQ):
                                        step(dve.tensor_scalar(
                                            r_rows[:, q, :], r_rows[:, q, :], r_mv[:, q, 0:1],
                                            r_rstd[:, q:q + 1], ALU.subtract, ALU.mult))
                                    step(dve.tensor_copy(r_hi[:], r_rows[:]))
                                    step(dve.tensor_tensor(r_lo[:], r_rows[:],
                                                           r_hi[:].bitcast(F32), ALU.subtract))
                                    for q in range(EQ):
                                        step(dve.tensor_scalar(
                                            r_oh[:, q, :], iota_sb[:],
                                            col_of_slot[:, bass.ds(g * EQ + q, 1)], None,
                                            ALU.is_equal))
                                    dve.nop().then_inc(R["split"], 1)
                                    dve.wait_ge(R["sums"], n + 1)
                                    for f in range(FT):
                                        dve.tensor_copy(r_sum[:, f, :], bank[4 + f][:, 0:GN])\
                                           .then_inc(R["vector"], 1)
                                        dve.wait_ge(R["vector"], n * VS + (steps[0] + 1 + f))
                                    dve.tensor_copy(r_cnt[:], bank[6][0:8, 0:GN])\
                                       .then_inc(R["out"], 1)
                                    dve.wait_ge(R["added"], n * 32 + 32)
                                    assert steps[0] + FT == VS

                    @block.tensor
                    def _(pe):
                        rounds = pe.value_load(rounds_sb[0:1, 0:1], min_val=1,
                                               max_val=E // CAP + 1)
                        with pe.If(rounds > 1):
                            with pe.Fori(0, rounds - 1) as r:
                                table_tensor(pe, TX, r)
                                with pe.Fori(0, NG) as g:
                                    n = r * NG + g
                                    pe.wait_ge(R["split"], n + r + 4)
                                    for f in range(FT):
                                        for q in range(EQ):
                                            for part, t in enumerate((r_hi, r_lo)):
                                                pe.matmul(bank[4 + f][:, 0:GN],
                                                          t[:, q, f * P:(f + 1) * P],
                                                          r_oh[:, q, :], start=q + part == 0,
                                                          stop=q == EQ - 1 and part == 1)
                                    for q in range(EQ):
                                        mm = pe.matmul(bank[6][0:8, 0:GN], ones_r[:],
                                                       r_oh[:, q, :], start=q == 0,
                                                       stop=q == EQ - 1)
                                    mm.then_inc(R["sums"], 1)

            T0 = TableSems("", 0)
            with nc.Block() as block:
                @block.vector
                def _(dve):
                    table_vector(dve, T0, 0, rank)

                @block.gpsimd
                def _(pool):
                    table_pool(pool, T0, 0)

                @block.tensor
                def _(pe):
                    table_tensor(pe, T0, 0)

        with ExitStack() as c2:
            x_sb = [sb(f"x_sb{h}", [SP_, NS, D], F32, c2) for h in range(2)]
            rows = [sb(f"rows{h}", [P, EQ, D], F32, c2) for h in range(2)]
            xb_sb = [sb(f"xb_sb{h}", [SP_, NS, D], F32, c2) for h in range(2)]
            slots = [sb(f"slots{h}", [P, EQ], I32, c2) for h in range(2)]
            cols = sb("cols", [P, EQ], F32, c2)
            out_sb = [sb(f"out_sb{h}", [SP_, NS, D], F32, c2) for h in range(2)]
            x1_sb = [sb(f"x1_sb{h}", [SP_, NS, D], F32, c2) for h in range(2)]
            e_hi = sb("e_hi", [P, EQ, D], F32R, c2)
            e_lo = sb("e_lo", [P, EQ, D], F32R, c2)
            e_oh = sb("e_oh", [P, EQ, GN], F32R, c2)
            xn_sb = sb("xn_sb", [SP_, NS, D], F32, c2)
            x1n_sb = sb("x1n_sb", [SP_, NS, D], F32, c2)
            xT_hi = sb("xT_hi", [P, FT, GN], F32R, c2)
            xT_lo = sb("xT_lo", [P, FT, GN], F32R, c2)
            ag_hi = sb("ag_hi", [P, FT, GN], F32R, c2)
            ag_lo = sb("ag_lo", [P, FT, GN], F32R, c2)
            x1T_hi = sb("x1T_hi", [P, FT, GN], F32R, c2)
            x1T_lo = sb("x1T_lo", [P, FT, GN], F32R, c2)
            h1f = [sb(f"h1f{t}", [P, GN], F32, c2) for t in range(NF1)]
            h1_hi = sb("h1_hi", [P, H1T, GN], F32R, c2)
            h1_lo = sb("h1_lo", [P, H1T, GN], F32R, c2)
            h2f = [sb(f"h2f{t}", [P, GN], F32, c2) for t in range(H2T)]
            h2_hi = sb("h2_hi", [P, H2T, GN], F32R, c2)
            h2_lo = sb("h2_lo", [P, H2T, GN], F32R, c2)
            cnt_sb = sb("cnt_sb", [8, GN], F32, c2)
            lgT_sb = sb("lgT_sb", [8, GN], F32, c2)
            wT_r = sb("wT_r", [NB3, GN], F32R, c2)
            e_st = sb("e_st", [P, EQ, 6], F32, c2)
            e_mv = sb("e_mv", [P, EQ, 2], F32, c2)
            e_var = sb("e_var", [P, EQ], F32, c2)
            e_rstd = sb("e_rstd", [P, EQ], F32, c2)
            e_nb = sb("e_nb", [P, EQ], F32, c2)
            ln = {}
            for k in (1, 2):
                ln[k] = dict(st=sb(f"l{k}_st", [SP_, NS, 6], F32, c2),
                             mv=sb(f"l{k}_mv", [SP_, NS, 2], F32, c2),
                             var=sb(f"l{k}_var", [SP_, NS], F32, c2),
                             rstd=sb(f"l{k}_rstd", [SP_, NS], F32, c2),
                             nb=sb(f"l{k}_nb", [SP_, NS], F32, c2))
            deg = sb("deg", [SP_, NS], F32, c2)
            inv_deg = sb("inv_deg", [SP_, NS], F32, c2)
            z = sb("z", [SP_, NS, NX], F32, c2)
            ga = sb("ga", [SP_, NS, NX], F32, c2)
            gd = sb("gd", [SP_, NS, NX], F32, c2)
            gy = sb("gy", [SP_, NS, NX], F32, c2)
            grank = sb("grank", [SP_, NS, NX], F32, c2)
            g1 = sb("g1", [SP_, NS], F32, c2)
            g2 = sb("g2", [SP_, NS], F32, c2)
            gpair = sb("gpair", [SP_, NS, NX, NX], F32, c2)
            wst = sb("wst", [SP_, NS, NB3], F32, c2)

            more_sb = sb("more_sb", [P, FT, GN], F32, c2)
            more_cnt = sb("more_cnt", [8, GN], F32, c2)
            agf_sb = sb("agf_sb", [P, FT, GN], F32, c2)
            s_more = sem("more_sums_loaded")
            s_agf = sem("all_sums_ready")

            x_v = x.rearrange("(g p s) d -> g p s d", p=SP_, s=NS)
            out_v = out.rearrange("(g p s) d -> g p s d", p=SP_, s=NS)

            s_x = [sem(f"x_loaded{h}") for h in range(2)]
            s_rows = [sem(f"rows_gathered{h}") for h in range(2)]
            s_store = [sem(f"out_stored{h}") for h in range(2)]
            names = ("slots_copied cols_copied e_st_ready e_mv_ready e_var_ready e_rstd_ready e_nb_ready e_norm_ready "
                     "e_hi_ready e_lo_ready e_oh_ready l1_st_ready l1_mv_ready l1_var_ready "
                     "l1_rstd_ready l1_nb_ready xn_ready xb_ready agg_done cnt_ready agg_hi_ready "
                     "agg_lo_ready xT_done xT_hi_ready xT_lo_ready cntT_done deg_ready inv_ready gnn_done "
                     "t_ready x1_ready l2_st_ready l2_mv_ready l2_var_ready l2_rstd_ready "
                     "x1n_ready x1T_done x1T_hi_ready x1T_lo_ready lg_done lgT_ready lgN_done "
                     "gate_step gates_own exp_ready gates_ready wT_done wT_ready l1_done h1_relu_ready "
                     "h1_hi_ready h1_lo_ready gate_bc_done l2_done h2_relu_ready h2_gated "
                     "h2_hi_ready h2_lo_ready l3_done out_ready rows_cleared").split()
            S = {n: sem(n) for n in names}

            class G:

                def __init__(self, k, c):
                    self.k, self.c = k, c
                    self.h = c % 2

                def __add__(self, d):
                    return G(self.k, self.c + d)

                def at(self):
                    return self.k * 2 + self.c

                def n(self, per, done=0):
                    return self.k * (2 * per) + (self.c * per + done)

                def dma(self, per):
                    return self.k * per + (self.c // 2 + 1) * per

            def layernorm_pool(pool, g, k, mv, tag, per):
                n = mv.shape[1]
                pn = mv.shape[0]
                wait_alone(pool, S[f"{tag}_mv_ready"], g.n(per, per))
                L = ln[k] if k else dict(var=e_var, rstd=e_rstd)
                pool.tensor_scalar(L["var"][:], mv[:, :, 1], EPS, None,
                                   ALU.add).then_inc(S[f"{tag}_var_ready"], 1)
                pool.wait_ge(S[f"{tag}_var_ready"], g.n(1, 1))
                if tag == "e":
                    pool.wait_ge(S["e_norm_ready"], g.n(EQ))
                elif tag == "l1":
                    pool.wait_ge(S["xn_ready"], g.n(NS))
                else:
                    pool.wait_ge(S["x1n_ready"], g.n(NS))
                pool.tensor_tensor(L["rstd"][:], L["var"][:], half_neg[0:pn, 0:n],
                                   ALU.pow).then_inc(S[f"{tag}_rstd_ready"], 1)

            def gather(pool, g):
                pool.wait_ge(S["e_lo_ready"], g.n(1, -1)) if g.c >= 2 else None
                if g.c >= 2:
                    pool.wait_ge(s_rows[g.h], (g + -2).dma(16 * EQ))
                pool.tensor_copy(slots[g.h][:], src_of_slot[:, bass.ds(g.at() * EQ, EQ)])\
                    .then_inc(S["slots_copied"], 1)
                wait_alone(pool, S["slots_copied"], g.n(1, 1))
                for q in range(EQ):
                    pool.indirect_dma_start(
                        out=rows[g.h][:, q, :], out_offset=None, in_=x,
                        in_offset=bass.IndirectOffsetOnAxis(ap=slots[g.h][:, q:q + 1], axis=0),
                        bounds_check=N - 1, oob_is_err=False).then_inc(s_rows[g.h], 16)

            def edges_vector_a(dve, g):
                dve.wait_ge(s_rows[g.h], g.dma(16 * EQ))
                dve.wait_ge(S["e_var_ready"], g.n(1)) if g.c else None
                for q in range(EQ):
                    dve.bn_stats(e_st[:, q, :], rows[g.h][:, q, :]).then_inc(S["e_st_ready"], 1)
                wait_alone(dve, S["e_st_ready"], g.n(EQ, EQ))
                for q in range(EQ):
                    dve.bn_aggr(e_mv[:, q, :], e_st[:, q, :]).then_inc(S["e_mv_ready"], 1)

            def edges_vector_nb(dve, g):
                dve.wait_ge(S["e_rstd_ready"], g.n(1, 1))
                dve.scalar_tensor_tensor(out=e_nb[:], in0=e_mv[:, :, 0], scalar=-1.0,
                                         in1=e_rstd[:], op0=ALU.mult,
                                         op1=ALU.mult).then_inc(S["e_nb_ready"], 1)

            def edges_pool_oh(pool, g):
                if g.c:
                    pool.wait_ge(S["e_oh_ready"], g.n(EQ))
                pool.tensor_copy(cols[:], col_of_slot[:, bass.ds(g.at() * EQ, EQ)])\
                    .then_inc(S["cols_copied"], 1)
                if g.c:
                    wait_alone(pool, S["agg_done"], g.n(3))
                wait_alone(pool, S["cols_copied"], g.n(1, 1))
                for q in range(EQ):
                    pool.tensor_scalar(e_oh[:, q, :], iota_sb[:], cols[:, q:q + 1], None,
                                       ALU.is_equal).then_inc(S["e_oh_ready"], 1)

            def edges_vector_lo(dve, g):
                dve.wait_ge(S["e_hi_ready"], g.n(1, 1))
                dve.tensor_tensor(e_lo[:], rows[g.h][:], e_hi[:].bitcast(F32),
                                  ALU.subtract).then_inc(S["e_lo_ready"], 1)

            def edges_scalar_norm(act, g):
                act.wait_ge(S["e_nb_ready"], g.n(1, 1))
                for q in range(EQ):
                    act.activation(rows[g.h][:, q, :], rows[g.h][:, q, :], ACT.Identity,
                                   bias=e_nb[:, q:q + 1],
                                   scale=e_rstd[:, q:q + 1]).then_inc(S["e_norm_ready"], 1)

            def edges_scalar_hi(act, g):
                act.wait_ge(S["e_norm_ready"], g.n(EQ, EQ))
                if g.c:
                    act.wait_ge(S["agg_done"], g.n(3))
                act.copy(e_hi[:], rows[g.h][:]).then_inc(S["e_hi_ready"], 1)

            def sum_edges(pe, g, f):
                for q in range(EQ):
                    for part, t in enumerate((e_hi, e_lo)):
                        mm = pe.matmul(bank[4 + f][:, 0:GN], t[:, q, f * P:(f + 1) * P],
                                       e_oh[:, q, :], start=q + part == 0,
                                       stop=q == EQ - 1 and part == 1)
                mm.then_inc(S["agg_done"], 1)

            def count_edges(pe, g):
                for q in range(EQ):
                    mm = pe.matmul(bank[6][0:8, 0:GN], ones_r[:], e_oh[:, q, :],
                                   start=q == 0, stop=q == EQ - 1)
                mm.then_inc(S["agg_done"], 1)

            def ln1_vector_a(dve, g):
                dve.wait_ge(s_x[g.h], g.dma(16))
                if g.c:
                    dve.wait_ge(S["l1_var_ready"], g.n(1))
                for s in range(NS):
                    dve.bn_stats(ln[1]["st"][:, s, :], x_sb[g.h][:, s, :])\
                       .then_inc(S["l1_st_ready"], 1)
                wait_alone(dve, S["l1_st_ready"], g.n(NS, NS))
                for s in range(NS):
                    dve.bn_aggr(ln[1]["mv"][:, s, :], ln[1]["st"][:, s, :])\
                       .then_inc(S["l1_mv_ready"], 1)

            def ln1_vector_nb(dve, g):
                dve.wait_ge(S["l1_rstd_ready"], g.n(1, 1))
                dve.scalar_tensor_tensor(out=ln[1]["nb"][:], in0=ln[1]["mv"][:, :, 0], scalar=-1.0,
                                         in1=ln[1]["rstd"][:], op0=ALU.mult,
                                         op1=ALU.mult).then_inc(S["l1_nb_ready"], 1)

            def ln1_scalar(act, g):
                act.wait_ge(S["l1_nb_ready"], g.n(1, 1))
                act.wait_ge(S["xT_done"], g.n(2)) if g.c else None
                for s in range(NS):
                    act.activation(xn_sb[:, s, :], x_sb[g.h][:, s, :], ACT.Identity,
                                   bias=ln[1]["nb"][:, s:s + 1],
                                   scale=ln[1]["rstd"][:, s:s + 1]).then_inc(S["xn_ready"], 1)

            def xb_pool(pool, g):
                pool.wait_ge(s_x[g.h], g.dma(16))
                if g.c >= 2:
                    pool.wait_ge(S["t_ready"], g.n(2, -2))
                pool.tensor_tensor(xb_sb[g.h][:], x_sb[g.h][:], bias12[0:SP_],
                                   ALU.add).then_inc(S["xb_ready"], 1)

            def to_hi(act, dst, g, f, b, done, ready):
                act.wait_ge(S[done], g.n(2 if done != "agg_done" else 3, f + 1))
                act.copy(dst[:, f, :], bank[b][:, 0:GN]).then_inc(S[ready], 1)

            def to_lo(dve, dst, hi, g, f, b, hi_ready, ready):
                dve.wait_ge(S[hi_ready], g.n(2, f + 1))
                dve.tensor_tensor(dst[:, f, :], bank[b][:, 0:GN], hi[:, f, :].bitcast(F32),
                                  ALU.subtract).then_inc(S[ready], 1)

            def transpose_nodes(pe, src_t, b0, g, done):
                for f in range(FT):
                    for s in range(NS):
                        mm = pe.transpose(bank[b0 + f][:, s * SP_:(s + 1) * SP_],
                                          src_t[:, s, f * P:(f + 1) * P],
                                          ident_sb[0:SP_, 0:SP_])
                    mm.then_inc(S[done], 1)

            PARTS = ((0, 0), (1, 0), (0, 1))

            def step_tensor(pe, i, front, back):
                g = i + 1
                if front:
                    if g.c:
                        pe.wait_ge(S["t_ready"], g.n(2))
                    pe.wait_ge(S["e_lo_ready"], g.n(1, 1))
                    pe.wait_ge(S["e_oh_ready"], g.n(EQ, EQ))
                    sum_edges(pe, g, 0)
                if back:
                    pe.wait_ge(S["x1n_ready"], i.n(NS, NS))
                    if i.c:
                        pe.wait_ge(S["h2_relu_ready"], i.n(H2T))
                    transpose_nodes(pe, x1n_sb, 0, i, "x1T_done")
                if front:
                    sum_edges(pe, g, 1)
                if i.c > 0:
                    pe.wait_ge(S["out_ready"], i.n(2))
                if front:
                    count_edges(pe, g)
                if back:
                    pe.wait_ge(S["x1T_lo_ready"], i.n(2, 2))
                    n = 0
                    for part, t in enumerate((x1T_hi, x1T_lo)):
                        for f in range(FT):
                            mm = pe.matmul(bank[7][0:8, 0:GN], gw_hl[:, part, f, :], t[:, f, :],
                                           start=n == 0, stop=n == 3)
                            n += 1
                    mm.then_inc(S["lg_done"], 1)
                if front:
                    pe.wait_ge(S["xn_ready"], g.n(NS, NS))
                    if g.c:
                        pe.wait_ge(S["x1_ready"], g.n(NS))
                    transpose_nodes(pe, xn_sb, 2, g, "xT_done")
                if back:
                    wait_alone(pe, S["lgT_ready"], i.n(1, 1))
                    for s in range(NS):
                        mm = pe.transpose(bank[7][0:SP_, s * 8:(s + 1) * 8],
                                          lgT_sb[:, s * SP_:(s + 1) * SP_], ident_sb[0:8, 0:8])
                    mm.then_inc(S["lgN_done"], 1)
                if front:
                    wait_alone(pe, S["cnt_ready"], g.n(1, 1))
                    for s in range(NS):
                        mm = pe.transpose(bank[6][0:SP_, s * 8:(s + 1) * 8],
                                          cnt_sb[:, s * SP_:(s + 1) * SP_], ident_sb[0:8, 0:8])
                    mm.then_inc(S["cntT_done"], 1)
                if back:
                    for t in range(H1T):
                        if t in (2, 3) and front:
                            pe.wait_ge(S["agg_lo_ready"], g.n(2, t - 1))
                        elif t >= 4:
                            pe.wait_ge(S["h1_relu_ready"], i.n(H1T, t - 3))
                        n = 0
                        for a, w in PARTS:
                            for f in range(FT):
                                mm = pe.matmul(bank[L1_BANKS[t]][:, 0:GN],
                                               wl1_hl[:, w, f, t * P:(t + 1) * P],
                                               (x1T_hi, x1T_lo)[a][:, f, :],
                                               start=n == 0, stop=n == 5)
                                n += 1
                        mm.then_inc(S["l1_done"], 1)
                    pe.wait_ge(S["gates_ready"], i.n(1, 1))
                    if front:
                        pe.wait_ge(S["deg_ready"], g.n(1, 1))
                    for s in range(NS):
                        mm = pe.transpose(bank[6][0:NB3, s * SP_:(s + 1) * SP_], wst[:, s, :],
                                          ident_sb[0:SP_, 0:SP_])
                    mm.then_inc(S["wT_done"], 1)

                def graph_layer(j):
                    for s in (2 * j, 2 * j + 1):
                        cols_ = slice(s * SP_, (s + 1) * SP_)
                        for b, hl, wt in ((4, (xT_hi, xT_lo), w1_hl), (2, (ag_hi, ag_lo), w2_hl)):
                            n = 0
                            o = bank[b + j][0:SP_, (s % 2) * D:(s % 2 + 1) * D]
                            for a, w in PARTS:
                                for f in range(FT):
                                    mm = pe.matmul(o, hl[a][:, f, cols_], wt[:, w, f, :],
                                                   start=n == 0, stop=n == 5)
                                    n += 1
                    mm.then_inc(S["gnn_done"], 1)

                if front:
                    pe.wait_ge(S["agg_lo_ready"], g.n(2, 2))
                    pe.wait_ge(S["xT_lo_ready"], g.n(2, 2))
                    if back:
                        pe.wait_ge(S["h1_relu_ready"], i.n(H1T, 4))
                    graph_layer(0)
                if back:
                    pe.wait_ge(S["wT_ready"], i.n(1, 1))
                    for t in range(2):
                        pe.matmul(bank[6 + t][:, 0:GN], selg_r[:, t, :], wT_r[:],
                                  start=True, stop=True).then_inc(S["gate_bc_done"], 1)
                    pe.wait_ge(S["h1_lo_ready"], i.n(H1T, H1T))
                    for t in range(H2T):
                        if t == 2:
                            pe.wait_ge(S["h2_relu_ready"], i.n(H2T, 1))
                        n = 0
                        for a, w in PARTS:
                            for e in range(2):
                                mm = pe.matmul(bank[t % 2][:, 0:GN], wl2_hl[:, w, 2 * t + e, :],
                                               (h1_hi, h1_lo)[a][:, 2 * t + e, :],
                                               start=n == 0, stop=n == 5)
                                n += 1
                        mm.then_inc(S["l2_done"], 1)
                if front:
                    graph_layer(1)
                if back:
                    pe.wait_ge(S["h2_lo_ready"], i.n(H2T, H2T))
                    for s in range(NS):
                        cols_ = slice(s * SP_, (s + 1) * SP_)
                        o = bank[6 + s // 2][0:SP_, (s % 2) * D:(s % 2 + 1) * D]
                        pe.matmul(o, wT_r[:, cols_], b3_r[:], start=True, stop=False)
                        n = 0
                        for t in range(H2T):
                            for a, w in PARTS:
                                mm = pe.matmul(o, (h2_hi, h2_lo)[a][:, t, cols_],
                                               wl3_hl[:, w, t, :], start=False,
                                               stop=n == 3 * H2T - 1)
                                n += 1
                        if s % 2:
                            mm.then_inc(S["l3_done"], 1)

            def step_scalar(act, i, more, front, back, prep):
                g, p = i + 1, i + 2

                def ag_high(f):
                    if f == 0 and g.c:
                        act.wait_ge(S["gnn_done"], g.n(2))
                    if more:
                        act.wait_ge(s_agf, g.n(FT, f + 1))
                        act.copy(ag_hi[:, f, :], agf_sb[:, f, :]).then_inc(S["agg_hi_ready"], 1)
                    else:
                        to_hi(act, ag_hi, g, f, 4 + f, "agg_done", "agg_hi_ready")
                if front:
                    ag_high(0)
                if back:
                    for f in range(FT):
                        to_hi(act, x1T_hi, i, f, f, "x1T_done", "x1T_hi_ready")
                if front:
                    ag_high(1)
                    if not more:
                        act.wait_ge(S["agg_done"], g.n(3, 3))
                        act.copy(cnt_sb[:], bank[6][0:8, 0:GN]).then_inc(S["cnt_ready"], 1)
                if back:
                    act.wait_ge(S["lg_done"], i.n(1, 1))
                    act.copy(lgT_sb[:], bank[7][0:8, 0:GN]).then_inc(S["lgT_ready"], 1)
                if front:
                    for f in range(FT):
                        to_hi(act, xT_hi, g, f, 2 + f, "xT_done", "xT_hi_ready")

                def h1_value(t):
                    act.wait_ge(S["l1_done"], i.n(H1T, t + 1))
                    if t >= NF1:
                        act.wait_ge(S["h1_lo_ready"], i.n(H1T, t + 1 - NF1))
                    elif i.c:
                        act.wait_ge(S["h1_lo_ready"], i.n(H1T))
                    act.activation(h1f[t % NF1][:], bank[L1_BANKS[t]][:, 0:GN], ACT.Relu,
                                   bias=bl1_sb[:, t:t + 1]).then_inc(S["h1_relu_ready"], 1)

                def h1_high(t):
                    act.wait_ge(S["h1_relu_ready"], i.n(H1T, t + 1))
                    if t == 0 and i.c:
                        act.wait_ge(S["l2_done"], i.n(H2T))
                    act.copy(h1_hi[:, t, :], h1f[t % NF1][:]).then_inc(S["h1_hi_ready"], 1)

                if back:
                    h1_value(0)
                    act.wait_ge(S["gate_step"], i.n(4, 3))
                    act.activation(ga[:], z[:], ACT.Exp).then_inc(S["exp_ready"], 1)
                    h1_value(1)
                    h1_high(0)
                    act.wait_ge(S["gate_step"], i.n(4, 4))
                    act.activation(gy[:], gd[:], ACT.Exp).then_inc(S["exp_ready"], 1)
                    for t in range(2, H1T):
                        h1_value(t)
                        h1_high(t - 1)
                    h1_high(H1T - 1)
                    act.wait_ge(S["wT_done"], i.n(1, 1))
                    act.copy(wT_r[:], bank[6][0:NB3, 0:GN]).then_inc(S["wT_ready"], 1)
                if prep:
                    edges_scalar_norm(act, p)
                if back:
                    for t in range(H2T):
                        act.wait_ge(S["l2_done"], i.n(H2T, t + 1))
                        if i.c:
                            act.wait_ge(S["h2_lo_ready"], i.n(H2T))
                        act.activation(h2f[t][:], bank[t % 2][:, 0:GN], ACT.Relu,
                                       bias=bl2_sb[:, t:t + 1]).then_inc(S["h2_relu_ready"], 1)
                    for t in range(H2T):
                        if t < 2:
                            act.wait_ge(S["h2_gated"], i.n(2, t + 1))
                        else:
                            act.wait_ge(S["h2_relu_ready"], i.n(H2T, H2T))
                        if i.c and t == 0:
                            act.wait_ge(S["l3_done"], i.n(2))
                        act.copy(h2_hi[:, t, :], h2f[t][:]).then_inc(S["h2_hi_ready"], 1)
                if prep:
                    edges_scalar_hi(act, p)
                    ln1_scalar(act, p)

            def gates_vector(dve, i):
                own = [0]
                NGS = 13

                def step(ins):
                    ins.then_inc(S["gates_own"], 1)
                    own[0] += 1
                    dve.wait_ge(S["gates_own"], i.n(NGS, own[0]))
                b4 = [SP_, NS, NX]
                dve.wait_ge(S["lgN_done"], i.n(1, 1))
                lg = bank[7][0:SP_, 0:NS * 8].rearrange("p (s k e) -> p s e k", s=NS, k=2)
                dve.tensor_reduce(z[:], lg, AX.X, ALU.add).then_inc(S["gate_step"], 1)
                dve.wait_ge(S["gate_step"], i.n(4, 1))
                dve.tensor_tensor(z[:], z[:], gb_sb[0:SP_].unsqueeze(1).to_broadcast(b4),
                                  ALU.add).then_inc(S["gate_step"], 1)
                dve.wait_ge(S["gate_step"], i.n(4, 2))
                step(dve.tensor_reduce(g1[:], z[:], AX.X, ALU.max))
                dve.tensor_tensor(z[:], z[:], g1[:].unsqueeze(2).to_broadcast(b4),
                                  ALU.subtract).then_inc(S["gate_step"], 1)
                dve.wait_ge(S["exp_ready"], i.n(2, 1))
                step(dve.tensor_reduce(g1[:], ga[:], AX.X, ALU.add))
                step(dve.reciprocal(g2[:], g1[:]))
                r = g2[:].unsqueeze(2).to_broadcast(b4)
                step(dve.tensor_tensor(ga[:], ga[:], r, ALU.mult))
                dve.tensor_tensor(gd[:], ga[:], r, ALU.subtract).then_inc(S["gate_step"], 1)
                b16 = [SP_, NS, NX, NX]
                step(dve.tensor_tensor(gpair[:], ga[:].unsqueeze(2).to_broadcast(b16),
                                       ga[:].unsqueeze(3).to_broadcast(b16), ALU.subtract))
                step(dve.tensor_tensor(gpair[:], gpair[:],
                                       tie_sb[0:SP_].unsqueeze(1).to_broadcast(b16), ALU.is_gt))
                step(dve.tensor_reduce(grank[:], gpair[:], AX.X, ALU.add))
                dve.wait_ge(S["exp_ready"], i.n(2, 2))
                step(dve.scalar_tensor_tensor(out=gd[:], in0=grank[:], scalar=1.5, in1=gy[:],
                                              op0=ALU.is_lt, op1=ALU.mult))
                step(dve.tensor_reduce(g1[:], gd[:], AX.X, ALU.add))
                step(dve.reciprocal(g2[:], g1[:]))
                if i.c:
                    dve.wait_ge(S["wT_done"], i.n(1))
                step(dve.tensor_tensor(gd[:], gd[:], r, ALU.mult))
                step(dve.tensor_copy(wst[:, :, 0:NX].bitcast(F32R), gd[:]))
                dve.tensor_copy(wst[:, :, 2 * NX:3 * NX].bitcast(F32R), gd[:])\
                   .then_inc(S["gates_own"], 1)
                dve.tensor_tensor(wst[:, :, NX:2 * NX], gd[:], wst[:, :, 0:NX],
                                  ALU.subtract).then_inc(S["gates_ready"], 1)
                assert own[0] + 1 == NGS

            def graph_vector(dve, g, j):
                L = ln[2]
                dve.wait_ge(S["gnn_done"], g.n(2, j + 1))
                dve.tensor_tensor(
                    x1_sb[g.h][:, 2 * j:2 * j + 2, :],
                    bank[4 + j][0:SP_, :].rearrange("p (s d) -> p s d", s=2),
                    xb_sb[g.h][:, 2 * j:2 * j + 2, :], ALU.add).then_inc(S["t_ready"], 1)
                dve.wait_ge(S["t_ready"], g.n(2, j + 1))
                for s in (2 * j, 2 * j + 1):
                    dve.scalar_tensor_tensor(
                        out=x1_sb[g.h][:, s, :],
                        in0=bank[2 + j][0:SP_, (s % 2) * D:(s % 2 + 1) * D],
                        scalar=inv_deg[:, s:s + 1], in1=x1_sb[g.h][:, s, :],
                        op0=ALU.mult, op1=ALU.add).then_inc(S["x1_ready"], 1)
                for s in (2 * j, 2 * j + 1):
                    dve.wait_ge(S["x1_ready"], g.n(NS, s + 1))
                    dve.bn_stats(L["st"][:, s, :], x1_sb[g.h][:, s, :])\
                       .then_inc(S["l2_st_ready"], 1)

            def step_vector(dve, i, more, front, back, prep):
                g, p = i + 1, i + 2

                def ag_low(f):
                    if more:
                        dve.wait_ge(S["agg_hi_ready"], g.n(2, f + 1))
                        dve.tensor_tensor(ag_lo[:, f, :], agf_sb[:, f, :],
                                          ag_hi[:, f, :].bitcast(F32),
                                          ALU.subtract).then_inc(S["agg_lo_ready"], 1)
                    else:
                        to_lo(dve, ag_lo, ag_hi, g, f, 4 + f, "agg_hi_ready", "agg_lo_ready")

                def add_more(f):
                    dve.wait_ge(s_more, g.n(32, 32))
                    dve.wait_ge(S["agg_done"], g.n(3, f + 1))
                    dve.tensor_tensor(agf_sb[:, f, :], bank[4 + f][:, 0:GN],
                                      more_sb[:, f, :], ALU.add).then_inc(s_agf, 1)
                if prep:
                    edges_vector_a(dve, p)
                if front:
                    if more:
                        add_more(0)
                    ag_low(0)
                if back:
                    for f in range(FT):
                        to_lo(dve, x1T_lo, x1T_hi, i, f, f, "x1T_hi_ready", "x1T_lo_ready")
                if front:
                    if more:
                        add_more(1)
                        dve.wait_ge(S["agg_done"], g.n(3, 3))
                        dve.tensor_tensor(cnt_sb[:], bank[6][0:8, 0:GN], more_cnt[:],
                                          ALU.add).then_inc(S["cnt_ready"], 1)
                    ag_low(1)
                    for f in range(FT):
                        to_lo(dve, xT_lo, xT_hi, g, f, 2 + f, "xT_hi_ready", "xT_lo_ready")
                    dve.wait_ge(S["cntT_done"], g.n(1, 1))
                    dve.tensor_scalar(deg[:], bank[6][0:SP_, 0:NS * 8]
                                      .rearrange("p (s k) -> p s k", s=NS)[:, :, 0], 1.0, None,
                                      ALU.max).then_inc(S["deg_ready"], 1)
                    dve.wait_ge(S["deg_ready"], g.n(1, 1))
                    dve.reciprocal(inv_deg[:], deg[:]).then_inc(S["inv_ready"], 1)

                def h1_low(t):
                    dve.wait_ge(S["h1_hi_ready"], i.n(H1T, t + 1))
                    dve.tensor_tensor(h1_lo[:, t, :], h1f[t % NF1][:],
                                      h1_hi[:, t, :].bitcast(F32),
                                      ALU.subtract).then_inc(S["h1_lo_ready"], 1)
                if back:
                    gates_vector(dve, i)
                if prep:
                    edges_vector_nb(dve, p)
                if back:
                    for t in range(H1T):
                        h1_low(t)
                if prep:
                    ln1_vector_a(dve, p)
                if front:
                    dve.wait_ge(S["xb_ready"], g.n(1, 1))
                    dve.wait_ge(S["inv_ready"], g.n(1, 1))
                    if g.c:
                        dve.wait_ge(S["l2_var_ready"], g.n(1))
                    graph_vector(dve, g, 0)
                if prep:
                    ln1_vector_nb(dve, p)
                if back:
                    for t in range(2):
                        dve.wait_ge(S["gate_bc_done"], i.n(2, t + 1))
                        dve.wait_ge(S["h2_relu_ready"], i.n(H2T, t + 1))
                        dve.tensor_tensor(h2f[t][:], h2f[t][:], bank[6 + t][:, 0:GN],
                                          ALU.mult).then_inc(S["h2_gated"], 1)
                    for t in range(H2T):
                        dve.wait_ge(S["h2_hi_ready"], i.n(H2T, t + 1))
                        dve.tensor_tensor(h2_lo[:, t, :], h2f[t][:],
                                          h2_hi[:, t, :].bitcast(F32),
                                          ALU.subtract).then_inc(S["h2_lo_ready"], 1)
                if front:
                    L = ln[2]
                    graph_vector(dve, g, 1)
                    for s in range(NS):
                        wait_alone(dve, S["l2_st_ready"], g.n(NS, s + 1))
                        dve.bn_aggr(L["mv"][:, s, :], L["st"][:, s, :])\
                           .then_inc(S["l2_mv_ready"], 1)
                if prep:
                    edges_vector_lo(dve, p)
                if front:
                    dve.wait_ge(S["l2_rstd_ready"], g.n(1, 1))
                    if g.c:
                        dve.wait_ge(S["x1T_done"], g.n(2))
                    for s in range(NS):
                        dve.tensor_scalar(x1n_sb[:, s, :], x1_sb[g.h][:, s, :],
                                          L["mv"][:, s, 0:1], L["rstd"][:, s:s + 1],
                                          ALU.subtract, ALU.mult).then_inc(S["x1n_ready"], 1)
                if back:
                    if i.c >= 2:
                        dve.wait_ge(s_store[i.h], (i + -2).dma(16))
                    for j in range(2):
                        dve.wait_ge(S["l3_done"], i.n(2, j + 1))
                        dve.tensor_tensor(
                            out_sb[i.h][:, 2 * j:2 * j + 2, :],
                            bank[6 + j][0:SP_, :].rearrange("p (s d) -> p s d", s=2),
                            x1_sb[i.h][:, 2 * j:2 * j + 2, :], ALU.add).then_inc(S["out_ready"], 1)

            def load_x(sp, g):
                if g.c >= 2:
                    sp.wait_ge(S["l1_st_ready"], g.n(NS, -NS))
                    sp.wait_ge(S["xn_ready"], g.n(NS, -NS))
                    sp.wait_ge(S["xb_ready"], g.n(1, -1))
                sp.dma_start(x_sb[g.h][:], x_v[bass.ds(g.at(), 1)][0] if not isinstance(g.k, int)
                             else x_v[g.at()]).then_inc(s_x[g.h], 16)

            def load_more(sp, g):
                if g.c:
                    sp.wait_ge(s_agf, g.n(FT))
                    sp.wait_ge(S["cnt_ready"], g.n(1))
                at = bass.ds(g.at(), 1)
                if isinstance(g.k, int):
                    at = slice(g.at(), g.at() + 1)
                sp.dma_start(more_sb[:].rearrange("p f n -> p (f n)"), agg_x[at][0])\
                  .then_inc(s_more, 16)
                sp.dma_start(more_cnt[:], cnt_x[at][0]).then_inc(s_more, 16)

            def step_sync(sp, i, more, back, load):
                if load:
                    load_x(sp, i + 3)
                if more and (not isinstance(i.k, int) or i.c + 2 < NG):
                    load_more(sp, i + 2)
                if back:
                    sp.wait_ge(S["out_ready"], i.n(2, 2))
                    sp.dma_start(out_v[bass.ds(i.at(), 1)][0] if not isinstance(i.k, int)
                                 else out_v[i.at()], out_sb[i.h][:]).then_inc(s_store[i.h], 16)

            def step_pool(pool, i, front, prep, load):
                if prep:
                    layernorm_pool(pool, i + 2, 0, e_mv, "e", EQ)
                    edges_pool_oh(pool, i + 2)
                if load:
                    gather(pool, i + 3)
                if prep:
                    layernorm_pool(pool, i + 2, 1, ln[1]["mv"], "l1", NS)
                    xb_pool(pool, i + 2)
                if front:
                    layernorm_pool(pool, i + 1, 2, ln[2]["mv"], "l2", NS)

            def steps(run, eng):
                run(eng, G(0, -1))
                run(eng, G(0, 0))
                run(eng, G(0, 1))
                run(eng, G(0, 2))
                with eng.Fori(0, (NG - 6) // 2) as k:
                    run(eng, G(k, 3))
                    run(eng, G(k, 4))
                for c in range(NG - 3, NG):
                    run(eng, G(0, c))

            def flags(i):
                if not isinstance(i.k, int):
                    return dict(front=True, back=True, prep=True, load=True)
                return dict(front=i.c + 1 < NG, back=i.c >= 0, prep=i.c + 2 < NG,
                            load=i.c + 3 < NG)

            def either(eng, program):
                rounds = eng.value_load(rounds_sb[0:1, 0:1], min_val=1, max_val=E // CAP + 1)
                with eng.If(rounds < 2):
                    program(False)
                with eng.If(rounds > 1):
                    program(True)

            with nc.Block() as block:
                @block.sync
                def _(sp):
                    def program(more):
                        load_x(sp, G(0, 0))
                        load_x(sp, G(0, 1))
                        if more:
                            load_more(sp, G(0, 0))

                        def run(e, i):
                            f = flags(i)
                            step_sync(e, i, more, f["back"], f["load"])
                        steps(run, sp)
                        for h in range(2):
                            sp.wait_ge(s_store[h], 16 * (NG // 2))
                    either(sp, program)

                @block.gpsimd
                def _(pool):
                    pool.wait_ge(S["rows_cleared"], 2)
                    gather(pool, G(0, 0))
                    gather(pool, G(0, 1))
                    layernorm_pool(pool, G(0, 0), 0, e_mv, "e", EQ)
                    edges_pool_oh(pool, G(0, 0))
                    layernorm_pool(pool, G(0, 0), 1, ln[1]["mv"], "l1", NS)
                    xb_pool(pool, G(0, 0))

                    def run(e, i):
                        f = flags(i)
                        step_pool(e, i, f["front"], f["prep"], f["load"])
                    steps(run, pool)

                @block.vector
                def _(dve):
                    for h in range(2):
                        dve.memset(rows[h][:], 0.0).then_inc(S["rows_cleared"], 1)
                    dve.memset(wst[:], 1.0).then_inc(S["rows_cleared"], 1)
                    dve.wait_ge(S["rows_cleared"], 3)

                    def program(more):
                        p = G(0, 0)
                        edges_vector_a(dve, p)
                        ln1_vector_a(dve, p)
                        edges_vector_nb(dve, p)
                        ln1_vector_nb(dve, p)
                        edges_vector_lo(dve, p)

                        def run(e, i):
                            f = flags(i)
                            step_vector(e, i, more, f["front"], f["back"], f["prep"])
                        steps(run, dve)
                    either(dve, program)

                @block.scalar
                def _(act):
                    def program(more):
                        edges_scalar_norm(act, G(0, 0))
                        edges_scalar_hi(act, G(0, 0))
                        ln1_scalar(act, G(0, 0))

                        def run(e, i):
                            f = flags(i)
                            step_scalar(e, i, more, f["front"], f["back"], f["prep"])
                        steps(run, act)
                    either(act, program)

                @block.tensor
                def _(pe):
                    def run(e, i):
                        f = flags(i)
                        step_tensor(e, i, f["front"], f["back"])
                    steps(run, pe)


def _rows(a):
    return np.ascontiguousarray(a)


def kernel(**inputs):
    import concourse.bacc as bacc
    from concourse.bass_utils import run_bass_kernel_spmd

    v = {k: np.asarray(a) for k, a in inputs.items()}
    f = "L0_ffn_"

    def tiles(w):
        return _rows(w.reshape(w.shape[0] // P, P, w.shape[1]).transpose(1, 0, 2))

    e1 = v[f + "eW1"]
    l1 = np.concatenate([e1[e] for e in range(NX)] + [v[f + "sW1"]], axis=1)
    e2 = v[f + "eW2"]
    half = np.zeros_like(e2[0])
    l2 = np.stack([np.concatenate([e2[e], half] if e % 2 == 0 else [half, e2[e]], axis=1)
                   for e in range(NX)] + [v[f + "sW2"][0:P], v[f + "sW2"][P:2 * P]], axis=1)
    l3 = np.concatenate([v[f + "eW3"].reshape(NX * 64, D), v[f + "sW3"]], axis=0)
    b1 = np.concatenate([v[f + "eb1"].reshape(-1), v[f + "sb1"]]).reshape(H1T, P).T
    b2 = np.concatenate([v[f + "eb2"].reshape(-1), v[f + "sb2"]]).reshape(H2T, P).T
    b3 = np.concatenate([v[f + "eb3"]] * 3 + [v[f + "sb3"][None]] * 2, axis=0)

    selg = np.zeros((NB3, 3, P), np.float32)
    for e in range(NX):
        for k in range(2):
            selg[k * NX + e, e // 2, (e % 2) * 64:(e % 2) * 64 + 64] = 1
    low = np.array([0] * 8 + [1] * 4 + [0, 1])
    selg[:, 2, 0] = 1 - low
    selg[:, 2, 1] = low
    tie = np.zeros((P, NX, NX), np.float32)
    for e in range(NX):
        tie[:, e, :e] = -1.1754944e-38
    named = {
        "x": v["x"], "src": v["src"].reshape(EP, EC), "dst": v["dst"].reshape(EP, EC),
        "w1t": tiles(v["L0_gnn_W1"].T), "w2t": tiles(v["L0_gnn_W2"].T),
        "b12": np.stack([v["L0_gnn_b1"], v["L0_gnn_b2"]]),
        "wl1": tiles(l1), "bl1": b1, "wl2": l2, "bl2": b2, "wl3": tiles(l3), "b3": b3,
        "gw": tiles(v[f + "gW"]), "gb": v[f + "gb"],
        "ident": np.eye(P, dtype=np.float32),
        "ident16": np.stack([np.eye(NG), 256 * np.eye(NG)], 1).astype(np.float16),
        "upper16": np.triu(np.ones((EP, EP)), 1).astype(np.float16),
        "iota16": np.tile(np.arange(GN), (P, 1)).astype(np.float16),
        "iota": np.tile(np.arange(1, GN + 1), (P, 1)).astype(np.float32),
        "selg": selg, "tie": tie,
    }
    nc = bacc.Bacc("TRN2", target_bir_lowering=False, num_devices=1)
    arrays, args = {}, {}
    for name, a in named.items():
        a = _rows(a)
        arrays["in_" + name] = a
        args[name] = nc.dram_tensor("in_" + name, a.shape, mybir.dt.from_np(a.dtype),
                                    kind="ExternalInput").ap()
    out = nc.dram_tensor("out", (N, D), F32, kind="ExternalOutput").ap()
    agg_x = nc.dram_tensor("agg_x", (NG, P, FT * GN), F32, kind="Internal").ap()
    cnt_x = nc.dram_tensor("cnt_x", (NG, 8, GN), F32, kind="Internal").ap()
    build(nc, out=out, agg_x=agg_x, cnt_x=cnt_x, **args)
    return run_bass_kernel_spmd(nc, [arrays], core_ids=[0]).results[0]["out"]
```

```python
from contextlib import ExitStack

import numpy as np

import concourse.bass as bass
from concourse import mybir

F32, F32R, F16, I32 = mybir.dt.float32, mybir.dt.float32r, mybir.dt.float16, mybir.dt.int32
ALU = mybir.AluOpType
ACT = mybir.ActivationFunctionType
AX = mybir.AxisListType

P = 128
N = 50000
E = 50000
D = 256
FT = D // P
GN = 500
NG = N // GN
SP_ = 125
NS = GN // SP_
EQ = 5
CAP = EQ * P
NT = NG * EQ
EP = 125
EC = E // EP
CB = 5
BK = 5
STR = BK * CB
NIT = EC // STR
UNR = 4
NTI = EC // (UNR * CB)
LR = 96
LOW = 32
F16_LO = 1024
HALF_SRC = 25000
NEG_UP = 2 ** 15 - HALF_SRC
NX = 4
H1T = 6
H2T = 3
NB3 = 14
NF1 = 4
L1_BANKS = (0, 1, 4, 5, 0, 1)
EPS = 1e-5
RND = 12582912.0


def build(nc, x, src, dst, w1t, w2t, b12, wl1, bl1, wl2, bl2, wl3, b3, gw, gb,
          ident, bases16, upper16, iota16, iota, selg, tie, out, agg_x, cnt_x):
    with ExitStack() as ctx:
        def sem(name):
            return ctx.enter_context(nc.semaphore(name))

        def sb(name, shape, dt, c=ctx):
            return c.enter_context(nc.sbuf_tensor(name, shape, dt))

        bank = [ctx.enter_context(nc.psum_tensor(f"bank{b}", [P, 512], F32)) for b in range(8)]

        ident_sb = sb("ident_sb", [P, P], F32)
        iota_sb = sb("iota_sb", [P, GN], F32)
        bias12 = sb("bias12", [P, NS, D], F32)
        bl1_sb = sb("bl1_sb", [P, H1T], F32)
        bl2_sb = sb("bl2_sb", [P, H2T], F32)
        gb_sb = sb("gb_sb", [P, NX], F32)
        tie_sb = sb("tie_sb", [P, NX, NX], F32)
        half_neg = sb("half_neg", [P, EQ], F32)
        ones_r = sb("ones_r", [P, 8], F32R)
        zeros_r = sb("zeros_r", [P, 8], F32R)
        w1_hl = sb("w1_hl", [P, 2, FT, D], F32R)
        w2_hl = sb("w2_hl", [P, 2, FT, D], F32R)
        wl1_hl = sb("wl1_hl", [P, 2, FT, H1T * P], F32R)
        wl2_hl = sb("wl2_hl", [P, 2, 6, P], F32R)
        wl3_hl = sb("wl3_hl", [P, 2, H2T, D], F32R)
        gw_hl = sb("gw_hl", [P, 2, FT, 8], F32R)
        b3_r = sb("b3_r", [NB3, D], F32R)
        selg_r = sb("selg_r", [NB3, 2, P], F32R)
        src_of_slot = sb("src_of_slot", [P, NT], I32)
        col_of_slot = sb("col_of_slot", [P, NT], F32)
        rounds_sb = sb("rounds_sb", [1, 1], I32)

        s_passed = sem("lone_waits_passed")
        def wait_alone(eng, on, value):
            eng.wait_ge(on, value)
            if not isinstance(value, int):
                eng.sem_inc(s_passed, 1)

        s_w = sem("weights_loaded")
        s_cst = sem("constants_loaded")
        s_edge_in = sem("edges_loaded")
        s_bs = sem("bias_ready")

        with ExitStack() as c0:
            stage = {}
            parts = (("w1", w1t, w1_hl, 1), ("w2", w2t, w2_hl, 1), ("wl1", wl1, wl1_hl, 1),
                     ("wl2", wl2, wl2_hl, 1), ("wl3", wl3, wl3_hl, 1))
            for nm, ap, hl, _ in parts:
                stage[nm] = sb("st_" + nm, [P, *hl.shape[2:]], F32, c0)
            st_gw = sb("st_gw", [P, FT, NX], F32, c0)
            st_b3 = sb("st_b3", [NB3, D], F32, c0)
            st_b3b = sb("st_b3b", [NB3, D], F32, c0)
            st_sel = sb("st_sel", [NB3, 3, P], F32, c0)
            st_b = sb("st_b", [P, 2, D], F32, c0)
            b3_hi = sb("b3_hi", [NB3, D], F32R, c0)
            b3_lo = sb("b3_lo", [NB3, D], F32, c0)
            s_hi = sem("weight_high_ready")
            s_lo = sem("weight_low_ready")

            with nc.Block() as block:
                @block.sync
                def _(sp):
                    for nm, ap, _, _ in parts:
                        sp.dma_start(stage[nm][:], ap).then_inc(s_w, 16)
                    sp.dma_start(st_gw[:], gw).then_inc(s_w, 16)
                    sp.dma_start(st_b3[:], b3).then_inc(s_w, 16)
                    sp.dma_start(st_sel[:], selg).then_inc(s_w, 16)
                    sp.dma_start(st_b[:], b12.partition_broadcast(P)).then_inc(s_w, 16)
                    sp.dma_start(ident_sb[:], ident).then_inc(s_cst, 16)
                    sp.dma_start(iota_sb[:], iota).then_inc(s_cst, 16)
                    sp.dma_start(bl1_sb[:], bl1).then_inc(s_cst, 16)
                    sp.dma_start(bl2_sb[:], bl2).then_inc(s_cst, 16)
                    sp.dma_start(gb_sb[:], gb.partition_broadcast(P)).then_inc(s_cst, 16)
                    sp.dma_start(tie_sb[:], tie).then_inc(s_cst, 16)

                @block.vector
                def _(dve):
                    dve.wait_ge(s_w, 16 * 9)
                    n = 0
                    for nm, _, hl, _ in parts:
                        dve.tensor_copy(hl[:, 0], stage[nm][:]).then_inc(s_hi, 1)
                        n += 1
                        dve.wait_ge(s_hi, n)
                        dve.tensor_tensor(hl[:, 1], stage[nm][:], hl[:, 0].bitcast(F32),
                                          ALU.subtract).then_inc(s_lo, 1)
                    dve.tensor_copy(gw_hl[:, 0, :, 0:NX], st_gw[:]).then_inc(s_hi, 1)
                    dve.tensor_copy(gw_hl[:, 1, :, 0:NX], st_gw[:]).then_inc(s_hi, 1)
                    dve.memset(gw_hl[:, 1, :, NX:8].bitcast(F32), 0.0).then_inc(s_lo, 1)
                    dve.wait_ge(s_hi, n + 2)
                    dve.tensor_tensor(gw_hl[:, 0, :, NX:8], st_gw[:],
                                      gw_hl[:, 0, :, 0:NX].bitcast(F32),
                                      ALU.subtract).then_inc(s_lo, 1)
                    dve.tensor_copy(b3_hi[:], st_b3[:]).then_inc(s_hi, 1)
                    dve.wait_ge(s_hi, n + 3)
                    dve.tensor_tensor(b3_lo[:], st_b3[:], b3_hi[:].bitcast(F32),
                                      ALU.subtract).then_inc(s_hi, 1)
                    dve.wait_ge(s_hi, n + 4)
                    dve.tensor_scalar(st_b3b[:], b3_lo[:], st_sel[:, 2, 1:2], None,
                                      ALU.mult).then_inc(s_hi, 1)
                    dve.wait_ge(s_hi, n + 5)
                    dve.scalar_tensor_tensor(out=b3_r[:], in0=b3_hi[:].bitcast(F32),
                                             scalar=st_sel[:, 2, 0:1], in1=st_b3b[:],
                                             op0=ALU.mult, op1=ALU.add).then_inc(s_lo, 1)
                    dve.tensor_copy(selg_r[:], st_sel[:, 0:2]).then_inc(s_lo, 1)
                    for s in range(NS):
                        dve.tensor_tensor(bias12[:, s], st_b[:, 0], st_b[:, 1],
                                          ALU.add).then_inc(s_bs, 1)
                    dve.memset(half_neg[:], -0.5).then_inc(s_bs, 1)
                    dve.memset(ones_r[:].bitcast(F32), 1.0).then_inc(s_bs, 1)
                    dve.memset(zeros_r[:].bitcast(F32), 0.0).then_inc(s_bs, 1)

        with ExitStack() as c1:
            up16 = sb("up16", [EP, EP + 1], F16, c1)
            base16 = sb("base16", [EP + 1, EP + 1], F16, c1)
            io16 = sb("io16", [P, GN], F16, c1)
            ones16 = sb("ones16", [EP, EP + 1], F16, c1)
            zero16 = sb("zero16", [EP, GN], F16, c1)
            ei = sb("ei", [EP, 2, EC], I32, c1)
            ef = sb("ef", [EP, 2, EC], F32, c1)
            t0 = sb("t0", [EP, EC], F32, c1)
            t1 = sb("t1", [EP, EC], F32, c1)
            t2 = sb("t2", [EP, EC], F32, c1)
            grp = sb("grp", [EP, EC], F32, c1)
            grp16 = sb("grp16", [EP, EC], F16, c1)
            src_pat = sb("src_pat", [EP, EC], I32, c1)
            src_val = sb("src_val", [EP, EC], F32, c1)
            col16 = sb("col16", [EP, EC], F16, c1)
            rank = sb("rank", [EP, EC], F32, c1)
            slot16 = sb("slot16", [EP, EC], F16, c1)
            tcol = sb("tcol", [EP, EC], F32, c1)
            tmax = sb("tmax", [1, 4], F32, c1)
            c_oh = ExitStack()
            oh = sb("oh", [EP, EC, NG], F16, c_oh)
            prod = sb("prod", [EP, BK, CB, NG], F32, c_oh)
            base = sb("base", [EP + 1, STR + 1, NG], F32, c_oh)
            base_t = sb("base_t", [EP + 1, STR, NG], F32, c_oh)
            base_hi = sb("base_hi", [EP + 1, STR, NG], F16, c_oh)
            run16 = sb("run16", [EP + 1, STR, NG], F16, c_oh)

            s_c = sem("sort_step")
            s_c0 = sem("sort_constants_loaded")
            s_oh = sem("group_onehots_ready")
            s_one = sem("ones_ready")
            s_tot = sem("stream_totals_ready")
            s_base = sem("stream_bases_ready")
            s_run = sem("running_prefix_ready")
            s_pre = sem("prefix_in_psum")
            s_prod = sem("prefix_selected")
            s_rank = sem("ranks_ready")

            def dve_steps(dve):
                count = [0]

                def step(ins):
                    ins.then_inc(s_c, 1)
                    count[0] += 1
                    dve.wait_ge(s_c, count[0])
                return step

            with nc.Block() as block:
                @block.sync
                def _(sp):
                    sp.dma_start(ei[:, 0], src).then_inc(s_edge_in, 16)
                    sp.dma_start(ei[:, 1], dst).then_inc(s_edge_in, 16)
                    sp.dma_start(io16[:], iota16).then_inc(s_c0, 16)
                    sp.dma_start(up16[:], upper16).then_inc(s_c0, 16)
                    sp.dma_start(base16[:], bases16).then_inc(s_c0, 16)

                @block.vector
                def _(dve):
                    step = dve_steps(dve)
                    dve.memset(ones16[:], 1.0).then_inc(s_one, 1)
                    dve.memset(zero16[:], 0.0).then_inc(s_one, 1)
                    dve.memset(base[:, 0], 0.0).then_inc(s_base, 1)
                    dve.wait_ge(s_edge_in, 32)
                    step(dve.tensor_copy(ef[:], ei[:]))
                    step(dve.tensor_scalar(t0[:], ef[:, 0], 1.0 / GN, -0.499, ALU.mult, ALU.add))
                    step(dve.tensor_scalar(grp[:], t0[:], RND, RND, ALU.add, ALU.subtract))
                    step(dve.tensor_copy(grp16[:], grp[:]))
                    dve.wait_ge(s_c0, 48)
                    for k in range(NIT):
                        a = slice(k * STR, (k + 1) * STR)
                        dve.tensor_tensor(
                            oh[:, a], grp16[:, a].unsqueeze(2).to_broadcast([EP, STR, NG]),
                            io16[0:EP, 0:NG].unsqueeze(1).to_broadcast([EP, STR, NG]),
                            ALU.is_equal).then_inc(s_oh, 1)
                    step(dve.scalar_tensor_tensor(out=t1[:], in0=grp[:], scalar=-float(GN),
                                                  in1=ef[:, 0], op0=ALU.mult, op1=ALU.add))
                    step(dve.tensor_scalar(t0[:], t1[:], 1.0 / NS, -0.375, ALU.mult, ALU.add))
                    step(dve.tensor_scalar(t2[:], t0[:], RND, RND, ALU.add, ALU.subtract))
                    step(dve.scalar_tensor_tensor(out=t0[:], in0=t2[:], scalar=-float(NS),
                                                  in1=t1[:], op0=ALU.mult, op1=ALU.add))
                    step(dve.tensor_scalar(t1[:], t0[:], float(SP_), 1.0, ALU.mult, ALU.add))
                    step(dve.tensor_tensor(col16[:], t1[:], t2[:], ALU.add))
                    step(dve.tensor_scalar(t0[:], ef[:, 1], HALF_SRC - 0.5, float(NEG_UP),
                                           ALU.is_gt, ALU.mult))
                    step(dve.tensor_tensor(t1[:], t0[:], ef[:, 1], ALU.add))
                    step(dve.tensor_scalar(t2[:], t1[:], float(F16_LO), None, ALU.add))
                    step(dve.tensor_copy(src_pat[:], t2[:]))
                    step(dve.tensor_copy(src_val[:], src_pat[:].bitcast(F16)[:, 0:2 * EC:2]))
                    dve.wait_ge(s_base, 1)
                    for s_ in range(STR):
                        dve.wait_ge(s_tot, s_ // CB + 1)
                        dve.tensor_tensor(
                            base[:, s_ + 1], base[:, s_],
                            bank[s_ // CB][0:EP + 1, (s_ % CB) * NG:(s_ % CB + 1) * NG],
                            ALU.add).then_inc(s_base, 1)
                        dve.wait_ge(s_base, s_ + 2)
                    step(dve.tensor_scalar(base_t[:], base[:, 0:STR], 1.0 / LOW, -0.49,
                                           ALU.mult, ALU.add))
                    step(dve.tensor_scalar(base_hi[:], base_t[:], RND, RND, ALU.add,
                                           ALU.subtract))
                    dve.tensor_copy(run16[0:LR], base_hi[0:LR]).then_inc(s_base, 1)
                    dve.scalar_tensor_tensor(out=run16[LR:EP + 1], in0=base_hi[LR:EP + 1],
                                             scalar=-float(LOW), in1=base[LR:EP + 1, 0:STR],
                                             op0=ALU.mult, op1=ALU.add).then_inc(s_run, BK)
                    dve.nop().then_inc(s_prod, BK)
                    with dve.Fori(0, NIT) as it:
                        def selected(b):
                            dve.wait_ge(s_prod, it * BK + (BK + b + 1))
                            dve.tensor_reduce(rank[:, bass.ds(it * STR + b * CB, CB)], prod[:, b],
                                              AX.X, ALU.add).then_inc(s_rank, 1)
                        for b in range(BK):
                            dve.wait_ge(s_run, it * BK + (BK + b + 1))
                            dve.tensor_tensor(
                                prod[:, b],
                                bank[b][0:EP, 0:CB * NG].rearrange("p (c g) -> p c g", c=CB),
                                oh[:, bass.ds(it * STR + b * CB, CB)], ALU.mult)\
                               .then_inc(s_prod, 1)
                            if b:
                                selected(b - 1)
                        selected(BK - 1)
                    dve.wait_ge(s_rank, NIT * BK)
                    step(dve.tensor_reduce(tmax[:, 0:1], base[0:1, STR], AX.X, ALU.max))
                    step(dve.tensor_scalar(tmax[:, 1:2], tmax[:, 0:1], 1.0 / CAP, 0.4995,
                                           ALU.mult, ALU.add))
                    step(dve.tensor_scalar(tmax[:, 2:3], tmax[:, 1:2], RND, RND, ALU.add,
                                           ALU.subtract))
                    step(dve.tensor_copy(rounds_sb[:], tmax[:, 2:3]))

                @block.tensor
                def _(pe):
                    def onehots(at):
                        return oh[:, bass.ds(at, CB)].rearrange("p c g -> p (c g)")

                    def totals(k, b, first, last):
                        return pe.matmul(bank[b][0:EP + 1, 0:CB * NG], ones16[:],
                                         onehots(k * STR + b * CB), start=first, stop=last)

                    pe.wait_ge(s_one, 2)
                    pe.wait_ge(s_oh, 1)
                    for b in range(BK):
                        totals(0, b, True, False)
                    with pe.Fori(0, NIT - 2) as it:
                        pe.wait_ge(s_oh, it + 2)
                        for b in range(BK):
                            totals(it + 1, b, False, False)
                    pe.wait_ge(s_oh, NIT)
                    for b in range(BK):
                        totals(NIT - 1, b, False, True).then_inc(s_tot, 1)
                    pe.wait_ge(s_c0, 48)
                    pe.wait_ge(s_base, STR + 2)
                    with pe.Fori(0, NIT) as it:
                        for b in range(BK):
                            n = it * BK + b
                            at = it * STR + b * CB
                            run = run16[:, b * CB:(b + 1) * CB].rearrange("p c g -> p (c g)")
                            o = bank[b][0:EP + 1, 0:CB * NG]
                            pe.wait_ge(s_prod, n + 1)
                            pe.wait_ge(s_run, n + 1)
                            pe.matmul(o, base16[:], run, start=True, stop=False)
                            pe.matmul(o, up16[:], onehots(at), start=False,
                                      stop=True).then_inc(s_pre, 1)

                @block.scalar
                def _(act):
                    with act.Fori(0, NIT) as it:
                        for b in range(BK):
                            act.wait_ge(s_pre, it * BK + (b + 1))
                            act.copy(run16[LR:EP + 1, b * CB:(b + 1) * CB]
                                     .rearrange("p c g -> p (c g)"),
                                     bank[b][LR:EP + 1, 0:CB * NG]).then_inc(s_run, 1)

            c_oh.close()
            rows1 = sb("slot_oh", [EP, UNR, CB, P], F16, c1)
            rowsv = sb("slot_val", [EP, UNR, 2, CB, P], F16, c1)
            cols1 = sb("cols1", [EP, UNR, CB, NT], F16, c1)
            tpat = sb("tpat", [P, NT], I32, c1)
            tsrc = sb("tsrc", [P, NT], F32, c1)
            tneg = sb("tneg", [P, NT], F32, c1)
            rank_r = sb("rank_r", [EP, EC], F32, c1)

            class TableSems:
                def __init__(self, tag, ahead):
                    self.ahead = ahead
                    self.step = sem(tag + "table_step")
                    self.row1 = sem(tag + "slot_onehots_ready")
                    self.rowv = sem(tag + "slot_sources_ready")
                    self.rowc = sem(tag + "slot_columns_ready")
                    self.col = sem(tag + "table_onehots_ready")
                    self.added = sem(tag + "table_chunks_added")
                    self.sums = sem(tag + "table_sums_done")
                    self.out = sem(tag + "table_written")

            NB = NTI * UNR

            def table_vector(dve, T, r, rk):
                steps = [0]

                def step(ins):
                    ins.then_inc(T.step, 1)
                    steps[0] += 1
                    if steps[0] < 7:
                        dve.wait_ge(T.step, r * 7 + steps[0])
                    else:
                        wait_alone(dve, T.step, r * 7 + 7)
                step(dve.tensor_scalar(t0[:], rk[:], 1.0 / P, -0.498, ALU.mult, ALU.add))
                step(dve.tensor_scalar(t1[:], t0[:], RND, RND, ALU.add, ALU.subtract))
                step(dve.scalar_tensor_tensor(out=t0[:], in0=t1[:], scalar=-float(P),
                                              in1=rk[:], op0=ALU.mult, op1=ALU.add))
                step(dve.tensor_scalar(t2[:], t1[:], 0.0, None, ALU.is_lt))
                step(dve.scalar_tensor_tensor(out=tcol[:], in0=t1[:], scalar=EQ - 0.5, in1=t2[:],
                                              op0=ALU.is_gt, op1=ALU.add))
                step(dve.scalar_tensor_tensor(out=slot16[:], in0=tcol[:], scalar=1000.0,
                                              in1=t0[:], op0=ALU.mult, op1=ALU.add))
                step(dve.scalar_tensor_tensor(out=tcol[:], in0=grp[:], scalar=float(EQ),
                                              in1=t1[:], op0=ALU.mult, op1=ALU.add))
                with dve.Fori(0, NTI) as it:
                    for u in range(UNR):
                        at = it * (UNR * CB) + u * CB
                        dve.wait_ge(T.added, r * (NB + UNR) + it * UNR + (u + 1))
                        dve.tensor_tensor(
                            rows1[:, u],
                            slot16[:, bass.ds(at, CB)].unsqueeze(2).to_broadcast([EP, CB, P]),
                            io16[0:EP, 0:P].unsqueeze(1).to_broadcast([EP, CB, P]),
                            ALU.is_equal).then_inc(T.row1, 1)
                        for j in range(CB):
                            ins = dve.tensor_scalar(cols1[:, u, j], io16[0:EP, 0:NT],
                                                    tcol[:, bass.ds(at + j, 1)], None,
                                                    ALU.is_equal)
                        ins.then_inc(T.col, 1)
                def last(ins, k):
                    ins.then_inc(T.out, 1)
                    dve.wait_ge(T.out, r * 9 + (k + T.ahead))
                dve.wait_ge(T.sums, r + 1)
                dve.tensor_copy(col_of_slot[:], bank[1][:, 0:NT]).then_inc(T.out, 1)
                last(dve.memset(tpat[:], 0), 2)
                last(dve.tensor_copy(tpat[:].bitcast(F16)[:, 0:2 * NT:2], bank[0][:, 0:NT]), 3)
                last(dve.tensor_copy(tsrc[:], tpat[:]), 4)
                last(dve.tensor_scalar(tneg[:], tsrc[:], 2.0 ** 15 - 0.5, -float(NEG_UP),
                                       ALU.is_gt, ALU.mult), 5)
                last(dve.scalar_tensor_tensor(out=tsrc[:], in0=tsrc[:], scalar=1.0 - F16_LO,
                                              in1=tneg[:], op0=ALU.add, op1=ALU.add), 6)
                last(dve.tensor_scalar(tneg[:], col_of_slot[:], 0.5, None, ALU.is_gt), 7)
                last(dve.tensor_tensor(tsrc[:], tsrc[:], tneg[:], ALU.mult), 8)
                dve.tensor_scalar(src_of_slot[:], tsrc[:], -1.0, None, ALU.add).then_inc(T.out, 1)

            def table_pool(pool, T, r):
                with pool.Fori(0, NTI) as it:
                    for u in range(UNR):
                        at = it * (UNR * CB) + u * CB
                        pool.wait_ge(T.row1, r * NB + it * UNR + (u + 1))
                        pool.tensor_tensor(
                            rowsv[:, u, 1], rows1[:, u],
                            col16[:, bass.ds(at, CB)].unsqueeze(2)
                            .to_broadcast([EP, CB, P]), ALU.mult).then_inc(T.rowc, 1)

            def table_scalar(act, T, r):
                with act.Fori(0, NTI) as it:
                    for u in range(UNR):
                        act.wait_ge(T.row1, r * NB + it * UNR + (u + 1))
                        for j in range(CB):
                            ins = act.activation(
                                rowsv[:, u, 0, j], rows1[:, u, j], ACT.Copy,
                                scale=src_val[:, bass.ds(it * (UNR * CB) + (u * CB + j), 1)])
                        ins.then_inc(T.rowv, 1)

            def table_tensor(pe, T, r):
                if not isinstance(r, int):
                    pe.wait_ge(T.out, r * 9 + T.ahead)
                for v in range(2):
                    mm = pe.matmul(bank[v][:, 0:NT], zero16[:, 0:P], zero16[:, 0:NT],
                                   start=True, stop=False)
                mm.then_inc(T.added, UNR)
                with pe.Fori(0, NTI) as it:
                    for u in range(UNR):
                        n = r * NB + it * UNR + (u + 1)
                        pe.wait_ge(T.col, n)
                        for v, ready in ((0, T.rowv), (1, T.rowc)):
                            pe.wait_ge(ready, n)
                            for j in range(CB):
                                mm = pe.matmul(bank[v][:, 0:NT], rowsv[:, u, v, j],
                                               cols1[:, u, j], start=False, stop=False)
                        mm.then_inc(T.added, 1)
                for v in range(2):
                    mm = pe.matmul(bank[v][:, 0:NT], zero16[:, 0:P], zero16[:, 0:NT],
                                   start=False, stop=True)
                mm.then_inc(T.sums, 1)

            with ExitStack() as cx:
                r_slots = sb("r_slots", [P, EQ], I32, cx)
                r_rows = sb("r_rows", [P, EQ, D], F32, cx)
                r_hi = sb("r_hi", [P, EQ, D], F32R, cx)
                r_lo = sb("r_lo", [P, EQ, D], F32R, cx)
                r_oh = sb("r_oh", [P, EQ, GN], F32R, cx)
                r_st = sb("r_st", [P, EQ, 6], F32, cx)
                r_mv = sb("r_mv", [P, EQ, 2], F32, cx)
                r_var = sb("r_var", [P, EQ], F32, cx)
                r_rstd = sb("r_rstd", [P, EQ], F32, cx)
                r_sum = sb("r_sum", [P, FT, GN], F32, cx)
                r_cnt = sb("r_cnt", [SP_, NS], F32, cx)
                VS = 4 * EQ + 2 + FT
                TX = TableSems("more_", 1)
                R = {n: sem("more_" + n) for n in
                     "zeros cleared slots gathered stats rstd vector split sums out added".split()}

                with nc.Block() as block:
                    @block.sync
                    def _(sp):
                        rounds = sp.value_load(rounds_sb[0:1, 0:1], min_val=1, max_val=E // CAP + 1)
                        with sp.If(rounds > 1):
                            sp.wait_ge(R["zeros"], 2)
                            with sp.Fori(0, NG) as g:
                                sp.dma_start(agg_x[bass.ds(g, 1)][0],
                                             r_sum[:].rearrange("p f n -> p (f n)"))\
                                  .then_inc(R["cleared"], 16)
                                sp.dma_start(cnt_x[bass.ds(g, 1)][0], r_cnt[:])\
                                  .then_inc(R["cleared"], 16)
                            sp.wait_ge(R["cleared"], 32 * NG)

                    @block.gpsimd
                    def _(pool):
                        rounds = pool.value_load(rounds_sb[0:1, 0:1], min_val=1,
                                                 max_val=E // CAP + 1)
                        with pool.If(rounds > 1):
                            pool.wait_ge(R["cleared"], 32 * NG)
                            with pool.Fori(0, rounds - 1) as r:
                                table_pool(pool, TX, r)
                                wait_alone(pool, TX.out, r * 9 + 10)
                                with pool.Fori(0, NG) as g:
                                    n = r * NG + g
                                    pool.tensor_copy(r_slots[:],
                                                     src_of_slot[:, bass.ds(g * EQ, EQ)])\
                                        .then_inc(R["slots"], 1)
                                    wait_alone(pool, R["slots"], n + 1)
                                    for q in range(EQ):
                                        pool.indirect_dma_start(
                                            out=r_rows[:, q, :], out_offset=None, in_=x,
                                            in_offset=bass.IndirectOffsetOnAxis(
                                                ap=r_slots[:, q:q + 1], axis=0),
                                            bounds_check=N - 1,
                                            oob_is_err=False).then_inc(R["gathered"], 16)
                                    wait_alone(pool, R["stats"], n + 1)
                                    pool.tensor_scalar(r_var[:], r_mv[:, :, 1], EPS, None,
                                                       ALU.add).then_inc(R["rstd"], 1)
                                    pool.wait_ge(R["rstd"], n * 2 + 1)
                                    pool.tensor_tensor(r_rstd[:], r_var[:], half_neg[:],
                                                       ALU.pow).then_inc(R["rstd"], 1)
                                    pool.wait_ge(R["out"], n + 1)
                                    pool.dma_start(agg_x[bass.ds(g, 1)][0],
                                                   r_sum[:].rearrange("p f n -> p (f n)"),
                                                   accum_op=ALU.add).then_inc(R["added"], 16)
                                    pool.dma_start(cnt_x[bass.ds(g, 1)][0], r_cnt[:],
                                                   accum_op=ALU.add).then_inc(R["added"], 16)
                                    wait_alone(pool, R["added"], n * 32 + 32)

                    @block.vector
                    def _(dve):
                        rounds = dve.value_load(rounds_sb[0:1, 0:1], min_val=1,
                                                max_val=E // CAP + 1)
                        with dve.If(rounds > 1):
                            dve.memset(r_sum[:], 0.0).then_inc(R["zeros"], 1)
                            dve.memset(r_cnt[:], 0.0).then_inc(R["zeros"], 1)
                            dve.memset(r_rows[:], 0.0).then_inc(R["split"], 1)
                            dve.tensor_copy(rank_r[:], rank[:]).then_inc(R["split"], 1)
                            dve.nop().then_inc(TX.out, 1)
                            dve.wait_ge(R["split"], 2)
                            with dve.Fori(0, rounds - 1) as r:
                                dve.tensor_scalar(rank_r[:], rank_r[:], -float(CAP), None,
                                                  ALU.add).then_inc(R["split"], 1)
                                dve.wait_ge(R["split"], r * (NG + 1) + 3)
                                table_vector(dve, TX, r, rank_r)
                                with dve.Fori(0, NG) as g:
                                    n = r * NG + g
                                    steps = [0]

                                    def step(ins, k=1):
                                        ins.then_inc(R["vector"], 1)
                                        steps[0] += 1
                                        if k:
                                            dve.wait_ge(R["vector"], n * VS + steps[0])
                                    dve.wait_ge(R["gathered"], n * (16 * EQ) + 16 * EQ)
                                    for q in range(EQ):
                                        step(dve.bn_stats(r_st[:, q, :], r_rows[:, q, :]), 0)
                                    wait_alone(dve, R["vector"], n * VS + EQ)
                                    for q in range(EQ):
                                        step(dve.bn_aggr(r_mv[:, q, :], r_st[:, q, :]), 0)
                                    dve.wait_ge(R["vector"], n * VS + 2 * EQ)
                                    dve.nop().then_inc(R["stats"], 1)
                                    dve.wait_ge(R["rstd"], n * 2 + 2)
                                    for q in range(EQ):
                                        step(dve.tensor_scalar(
                                            r_rows[:, q, :], r_rows[:, q, :], r_mv[:, q, 0:1],
                                            r_rstd[:, q:q + 1], ALU.subtract, ALU.mult))
                                    step(dve.tensor_copy(r_hi[:], r_rows[:]))
                                    step(dve.tensor_tensor(r_lo[:], r_rows[:],
                                                           r_hi[:].bitcast(F32), ALU.subtract))
                                    for q in range(EQ):
                                        step(dve.tensor_scalar(
                                            r_oh[:, q, :], iota_sb[:],
                                            col_of_slot[:, bass.ds(g * EQ + q, 1)], None,
                                            ALU.is_equal))
                                    dve.nop().then_inc(R["split"], 1)
                                    dve.wait_ge(R["sums"], n + 1)
                                    for f in range(FT):
                                        dve.tensor_copy(r_sum[:, f, :], bank[4 + f][:, 0:GN])\
                                           .then_inc(R["vector"], 1)
                                        dve.wait_ge(R["vector"], n * VS + (steps[0] + 1 + f))
                                    dve.tensor_copy(r_cnt[:], bank[6][0:SP_, 0:NS * 8]
                                                    .rearrange("p (s k) -> p s k", s=NS)[:, :, 0])\
                                       .then_inc(R["out"], 1)
                                    dve.wait_ge(R["added"], n * 32 + 32)
                                    assert steps[0] + FT == VS

                    @block.tensor
                    def _(pe):
                        rounds = pe.value_load(rounds_sb[0:1, 0:1], min_val=1,
                                               max_val=E // CAP + 1)
                        with pe.If(rounds > 1):
                            with pe.Fori(0, rounds - 1) as r:
                                table_tensor(pe, TX, r)
                                with pe.Fori(0, NG) as g:
                                    n = r * NG + g
                                    pe.wait_ge(R["split"], n + r + 4)
                                    for f in range(FT):
                                        for q in range(EQ):
                                            for part, t in enumerate((r_hi, r_lo)):
                                                pe.matmul(bank[4 + f][:, 0:GN],
                                                          t[:, q, f * P:(f + 1) * P],
                                                          r_oh[:, q, :], start=q + part == 0,
                                                          stop=q == EQ - 1 and part == 1)
                                    for s in range(NS):
                                        for q in range(EQ):
                                            mm = pe.matmul(
                                                bank[6][0:SP_, s * 8:(s + 1) * 8],
                                                r_oh[:, q, s * SP_:(s + 1) * SP_], ones_r[:],
                                                start=q == 0, stop=q == EQ - 1)
                                    mm.then_inc(R["sums"], 1)

                    @block.scalar
                    def _(act):
                        rounds = act.value_load(rounds_sb[0:1, 0:1], min_val=1,
                                                max_val=E // CAP + 1)
                        with act.If(rounds > 1):
                            with act.Fori(0, rounds - 1) as r:
                                table_scalar(act, TX, r)

            T0 = TableSems("", 0)
            with nc.Block() as block:
                @block.vector
                def _(dve):
                    table_vector(dve, T0, 0, rank)

                @block.gpsimd
                def _(pool):
                    table_pool(pool, T0, 0)

                @block.scalar
                def _(act):
                    table_scalar(act, T0, 0)

                @block.tensor
                def _(pe):
                    table_tensor(pe, T0, 0)

        with ExitStack() as c2:
            x_sb = [sb(f"x_sb{h}", [SP_, NS, D], F32, c2) for h in range(2)]
            rows = [sb(f"rows{h}", [P, EQ, D], F32, c2) for h in range(2)]
            xb_sb = [sb(f"xb_sb{h}", [SP_, NS, D], F32, c2) for h in range(2)]
            slots = [sb(f"slots{h}", [P, EQ], I32, c2) for h in range(2)]
            cols = sb("cols", [P, EQ], F32, c2)
            out_sb = [sb(f"out_sb{h}", [SP_, NS, D], F32, c2) for h in range(2)]
            x1_sb = [sb(f"x1_sb{h}", [SP_, NS, D], F32, c2) for h in range(2)]
            e_hi = sb("e_hi", [P, EQ, D], F32R, c2)
            e_lo = sb("e_lo", [P, EQ, D], F32R, c2)
            e_oh = sb("e_oh", [P, EQ, GN], F32R, c2)
            xn_sb = sb("xn_sb", [SP_, NS, D], F32, c2)
            x1n_sb = sb("x1n_sb", [SP_, NS, D], F32, c2)
            xT_hi = sb("xT_hi", [P, FT, GN], F32R, c2)
            xT_lo = sb("xT_lo", [P, FT, GN], F32R, c2)
            ag_hi = sb("ag_hi", [P, FT, GN], F32R, c2)
            ag_lo = sb("ag_lo", [P, FT, GN], F32R, c2)
            x1T_hi = sb("x1T_hi", [P, FT, GN], F32R, c2)
            x1T_lo = sb("x1T_lo", [P, FT, GN], F32R, c2)
            h1f = [sb(f"h1f{t}", [P, GN], F32, c2) for t in range(NF1)]
            h1_hi = sb("h1_hi", [P, H1T, GN], F32R, c2)
            h1_lo = sb("h1_lo", [P, H1T, GN], F32R, c2)
            h2f = [sb(f"h2f{t}", [P, GN], F32, c2) for t in range(H2T)]
            h2_hi = sb("h2_hi", [P, H2T, GN], F32R, c2)
            h2_lo = sb("h2_lo", [P, H2T, GN], F32R, c2)
            cnt_sb = sb("cnt_sb", [SP_, NS], F32, c2)
            oh_pair = sb("oh_pair", [P, 2, GN], F16, c2)
            oh_four = sb("oh_four", [P, GN], F16, c2)
            oh_sum = sb("oh_sum", [P, GN], F16, c2)
            one16 = sb("one16", [P, 1], F16, c2)
            lgT_sb = sb("lgT_sb", [8, GN], F32, c2)
            wT_r = sb("wT_r", [NB3, GN], F32R, c2)
            e_st = sb("e_st", [P, EQ, 6], F32, c2)
            e_mv = sb("e_mv", [P, EQ, 2], F32, c2)
            e_var = sb("e_var", [P, EQ], F32, c2)
            e_rstd = sb("e_rstd", [P, EQ], F32, c2)
            e_nb = sb("e_nb", [P, EQ], F32, c2)
            ln = {}
            for k in (1, 2):
                ln[k] = dict(st=sb(f"l{k}_st", [SP_, NS, 6], F32, c2),
                             mv=sb(f"l{k}_mv", [SP_, NS, 2], F32, c2),
                             var=sb(f"l{k}_var", [SP_, NS], F32, c2),
                             rstd=sb(f"l{k}_rstd", [SP_, NS], F32, c2),
                             nb=sb(f"l{k}_nb", [SP_, NS], F32, c2))
            deg = sb("deg", [SP_, NS], F32, c2)
            inv_deg = sb("inv_deg", [SP_, NS], F32, c2)
            z = sb("z", [SP_, NS, NX], F32, c2)
            ga = sb("ga", [SP_, NS, NX], F32, c2)
            gd = sb("gd", [SP_, NS, NX], F32, c2)
            gy = sb("gy", [SP_, NS, NX], F32, c2)
            grank = sb("grank", [SP_, NS, NX], F32, c2)
            g1 = sb("g1", [SP_, NS], F32, c2)
            g2 = sb("g2", [SP_, NS], F32, c2)
            gpair = sb("gpair", [SP_, NS, NX, NX], F32, c2)
            wst = sb("wst", [SP_, NS, NB3], F32, c2)

            more_sb = sb("more_sb", [P, FT, GN], F32, c2)
            more_cnt = sb("more_cnt", [SP_, NS], F32, c2)
            agf_sb = sb("agf_sb", [P, FT, GN], F32, c2)
            s_more = sem("more_sums_loaded")
            s_agf = sem("all_sums_ready")

            x_v = x.rearrange("(g p s) d -> g p s d", p=SP_, s=NS)
            out_v = out.rearrange("(g p s) d -> g p s d", p=SP_, s=NS)

            s_x = [sem(f"x_loaded{h}") for h in range(2)]
            s_rows = [sem(f"rows_gathered{h}") for h in range(2)]
            s_store = [sem(f"out_stored{h}") for h in range(2)]
            names = ("slots_copied cols_copied e_st_ready e_mv_ready e_var_ready e_rstd_ready e_nb_ready e_norm_ready "
                     "e_hi_ready e_lo_ready e_oh_ready oh_sum_ready l1_st_ready l1_mv_ready l1_var_ready "
                     "l1_rstd_ready l1_nb_ready xn_ready xb_ready agg_done cnt_ready agg_hi_ready "
                     "agg_lo_ready xT_done xT_hi_ready xT_lo_ready deg_ready inv_ready gnn_done "
                     "t_ready x1_ready l2_st_ready l2_mv_ready l2_var_ready l2_rstd_ready "
                     "x1n_ready x1T_done x1T_hi_ready x1T_lo_ready lg_done lgT_ready lgN_done "
                     "gate_step gates_own exp_ready gates_ready wT_done wT_ready l1_done h1_relu_ready "
                     "h1_hi_ready h1_lo_ready gate_bc_done l2_done h2_relu_ready h2_gated "
                     "h2_hi_ready h2_lo_ready l3_done out_ready rows_cleared").split()
            S = {n: sem(n) for n in names}

            class G:

                def __init__(self, k, c):
                    self.k, self.c = k, c
                    self.h = c % 2

                def __add__(self, d):
                    return G(self.k, self.c + d)

                def at(self):
                    return self.k * 2 + self.c

                def n(self, per, done=0):
                    return self.k * (2 * per) + (self.c * per + done)

                def dma(self, per):
                    return self.k * per + (self.c // 2 + 1) * per

            def layernorm_pool(pool, g, k, mv, tag, per):
                n = mv.shape[1]
                pn = mv.shape[0]
                wait_alone(pool, S[f"{tag}_mv_ready"], g.n(per, per))
                L = ln[k] if k else dict(var=e_var, rstd=e_rstd)
                pool.tensor_scalar(L["var"][:], mv[:, :, 1], EPS, None,
                                   ALU.add).then_inc(S[f"{tag}_var_ready"], 1)
                pool.wait_ge(S[f"{tag}_var_ready"], g.n(1, 1))
                if tag == "e":
                    pool.wait_ge(S["e_norm_ready"], g.n(EQ))
                elif tag == "l1":
                    pool.wait_ge(S["xn_ready"], g.n(NS))
                else:
                    pool.wait_ge(S["x1n_ready"], g.n(NS))
                pool.tensor_tensor(L["rstd"][:], L["var"][:], half_neg[0:pn, 0:n],
                                   ALU.pow).then_inc(S[f"{tag}_rstd_ready"], 1)

            def gather(pool, g):
                pool.wait_ge(S["e_lo_ready"], g.n(1, -1)) if g.c >= 2 else None
                if g.c >= 2:
                    pool.wait_ge(s_rows[g.h], (g + -2).dma(16 * EQ))
                pool.tensor_copy(slots[g.h][:], src_of_slot[:, bass.ds(g.at() * EQ, EQ)])\
                    .then_inc(S["slots_copied"], 1)
                wait_alone(pool, S["slots_copied"], g.n(1, 1))
                for q in range(EQ):
                    pool.indirect_dma_start(
                        out=rows[g.h][:, q, :], out_offset=None, in_=x,
                        in_offset=bass.IndirectOffsetOnAxis(ap=slots[g.h][:, q:q + 1], axis=0),
                        bounds_check=N - 1, oob_is_err=False).then_inc(s_rows[g.h], 16)

            def edges_vector_a(dve, g):
                dve.wait_ge(s_rows[g.h], g.dma(16 * EQ))
                dve.wait_ge(S["e_var_ready"], g.n(1)) if g.c else None
                for q in range(EQ):
                    dve.bn_stats(e_st[:, q, :], rows[g.h][:, q, :]).then_inc(S["e_st_ready"], 1)
                wait_alone(dve, S["e_st_ready"], g.n(EQ, EQ))
                for q in range(EQ):
                    dve.bn_aggr(e_mv[:, q, :], e_st[:, q, :]).then_inc(S["e_mv_ready"], 1)

            def edges_vector_nb(dve, g):
                dve.wait_ge(S["e_rstd_ready"], g.n(1, 1))
                dve.scalar_tensor_tensor(out=e_nb[:], in0=e_mv[:, :, 0], scalar=-1.0,
                                         in1=e_rstd[:], op0=ALU.mult,
                                         op1=ALU.mult).then_inc(S["e_nb_ready"], 1)

            def edges_pool_oh(pool, g):
                if g.c:
                    pool.wait_ge(S["e_oh_ready"], g.n(EQ))
                pool.tensor_copy(cols[:], col_of_slot[:, bass.ds(g.at() * EQ, EQ)])\
                    .then_inc(S["cols_copied"], 1)
                if g.c:
                    wait_alone(pool, S["agg_done"], g.n(3))
                wait_alone(pool, S["cols_copied"], g.n(1, 1))
                for q in range(EQ):
                    pool.tensor_scalar(e_oh[:, q, :], iota_sb[:], cols[:, q:q + 1], None,
                                       ALU.is_equal).then_inc(S["e_oh_ready"], 1)

            def edges_pool_sum(pool, g):
                pool.wait_ge(S["e_oh_ready"], g.n(EQ, EQ))
                pool.tensor_tensor(oh_pair[:], e_oh[:, 0:2].bitcast(F32),
                                   e_oh[:, 2:4].bitcast(F32),
                                   ALU.add).then_inc(S["oh_sum_ready"], 1)
                pool.wait_ge(S["oh_sum_ready"], g.n(3, 1))
                pool.tensor_tensor(oh_four[:], oh_pair[:, 0], oh_pair[:, 1],
                                   ALU.add).then_inc(S["oh_sum_ready"], 1)
                pool.wait_ge(S["oh_sum_ready"], g.n(3, 2))
                if g.c:
                    pool.wait_ge(S["agg_done"], g.n(3))
                pool.tensor_tensor(oh_sum[:], e_oh[:, 4].bitcast(F32), oh_four[:],
                                   ALU.add).then_inc(S["oh_sum_ready"], 1)

            def edges_vector_lo(dve, g):
                dve.wait_ge(S["e_hi_ready"], g.n(1, 1))
                dve.tensor_tensor(e_lo[:], rows[g.h][:], e_hi[:].bitcast(F32),
                                  ALU.subtract).then_inc(S["e_lo_ready"], 1)

            def edges_scalar_norm(act, g):
                act.wait_ge(S["e_nb_ready"], g.n(1, 1))
                for q in range(EQ):
                    act.activation(rows[g.h][:, q, :], rows[g.h][:, q, :], ACT.Identity,
                                   bias=e_nb[:, q:q + 1],
                                   scale=e_rstd[:, q:q + 1]).then_inc(S["e_norm_ready"], 1)

            def edges_scalar_hi(act, g):
                act.wait_ge(S["e_norm_ready"], g.n(EQ, EQ))
                if g.c:
                    act.wait_ge(S["agg_done"], g.n(3))
                act.copy(e_hi[:], rows[g.h][:]).then_inc(S["e_hi_ready"], 1)

            def sum_edges(pe, g, f):
                for q in range(EQ):
                    for part, t in enumerate((e_hi, e_lo)):
                        mm = pe.matmul(bank[4 + f][:, 0:GN], t[:, q, f * P:(f + 1) * P],
                                       e_oh[:, q, :], start=q + part == 0,
                                       stop=q == EQ - 1 and part == 1)
                mm.then_inc(S["agg_done"], 1)

            def count_edges(pe, g):
                pe.wait_ge(S["oh_sum_ready"], g.n(3, 3))
                for s in range(NS):
                    mm = pe.matmul(bank[6][0:SP_, s:s + 1], oh_sum[:, s * SP_:(s + 1) * SP_],
                                   one16[:], start=True, stop=True)
                mm.then_inc(S["agg_done"], 1)

            def ln1_vector_a(dve, g):
                dve.wait_ge(s_x[g.h], g.dma(16))
                if g.c:
                    dve.wait_ge(S["l1_var_ready"], g.n(1))
                for s in range(NS):
                    dve.bn_stats(ln[1]["st"][:, s, :], x_sb[g.h][:, s, :])\
                       .then_inc(S["l1_st_ready"], 1)
                wait_alone(dve, S["l1_st_ready"], g.n(NS, NS))
                for s in range(NS):
                    dve.bn_aggr(ln[1]["mv"][:, s, :], ln[1]["st"][:, s, :])\
                       .then_inc(S["l1_mv_ready"], 1)

            def ln1_vector_nb(dve, g):
                dve.wait_ge(S["l1_rstd_ready"], g.n(1, 1))
                dve.scalar_tensor_tensor(out=ln[1]["nb"][:], in0=ln[1]["mv"][:, :, 0], scalar=-1.0,
                                         in1=ln[1]["rstd"][:], op0=ALU.mult,
                                         op1=ALU.mult).then_inc(S["l1_nb_ready"], 1)

            def ln1_scalar(act, g):
                act.wait_ge(S["l1_nb_ready"], g.n(1, 1))
                act.wait_ge(S["xT_done"], g.n(2)) if g.c else None
                for s in range(NS):
                    act.activation(xn_sb[:, s, :], x_sb[g.h][:, s, :], ACT.Identity,
                                   bias=ln[1]["nb"][:, s:s + 1],
                                   scale=ln[1]["rstd"][:, s:s + 1]).then_inc(S["xn_ready"], 1)

            def xb_pool(pool, g):
                pool.wait_ge(s_x[g.h], g.dma(16))
                if g.c >= 2:
                    pool.wait_ge(S["t_ready"], g.n(2, -2))
                pool.tensor_tensor(xb_sb[g.h][:], x_sb[g.h][:], bias12[0:SP_],
                                   ALU.add).then_inc(S["xb_ready"], 1)

            def to_hi(act, dst, g, f, b, done, ready):
                act.wait_ge(S[done], g.n(2 if done != "agg_done" else 3, f + 1))
                act.copy(dst[:, f, :], bank[b][:, 0:GN]).then_inc(S[ready], 1)

            def to_lo(dve, dst, hi, g, f, b, hi_ready, ready):
                dve.wait_ge(S[hi_ready], g.n(2, f + 1))
                dve.tensor_tensor(dst[:, f, :], bank[b][:, 0:GN], hi[:, f, :].bitcast(F32),
                                  ALU.subtract).then_inc(S[ready], 1)

            def transpose_nodes(pe, src_t, b0, g, done):
                for f in range(FT):
                    for s in range(NS):
                        mm = pe.transpose(bank[b0 + f][:, s * SP_:(s + 1) * SP_],
                                          src_t[:, s, f * P:(f + 1) * P],
                                          ident_sb[0:SP_, 0:SP_])
                    mm.then_inc(S[done], 1)

            PARTS = ((0, 0), (1, 0), (0, 1))

            def step_tensor(pe, i, front, back):
                g = i + 1
                if front:
                    if g.c:
                        pe.wait_ge(S["t_ready"], g.n(2))
                    pe.wait_ge(S["e_lo_ready"], g.n(1, 1))
                    pe.wait_ge(S["e_oh_ready"], g.n(EQ, EQ))
                    sum_edges(pe, g, 0)
                if back:
                    pe.wait_ge(S["x1n_ready"], i.n(NS, NS))
                    if i.c:
                        pe.wait_ge(S["h2_relu_ready"], i.n(H2T))
                    transpose_nodes(pe, x1n_sb, 0, i, "x1T_done")
                if front:
                    sum_edges(pe, g, 1)
                if i.c > 0:
                    pe.wait_ge(S["out_ready"], i.n(2))
                if front:
                    count_edges(pe, g)
                if back:
                    n = 0
                    for part, t in enumerate((x1T_hi, x1T_lo)):
                        pe.wait_ge(S[("x1T_hi_ready", "x1T_lo_ready")[part]], i.n(2, 2))
                        for f in range(FT):
                            mm = pe.matmul(bank[7][0:8, 0:GN], gw_hl[:, part, f, :], t[:, f, :],
                                           start=n == 0, stop=n == 3)
                            n += 1
                    mm.then_inc(S["lg_done"], 1)
                if front:
                    pe.wait_ge(S["xn_ready"], g.n(NS, NS))
                    if g.c:
                        pe.wait_ge(S["x1_ready"], g.n(NS))
                    transpose_nodes(pe, xn_sb, 2, g, "xT_done")
                if back:
                    wait_alone(pe, S["lgT_ready"], i.n(1, 1))
                    for s in range(NS):
                        mm = pe.transpose(bank[7][0:SP_, s * 8:(s + 1) * 8],
                                          lgT_sb[:, s * SP_:(s + 1) * SP_], ident_sb[0:8, 0:8])
                    mm.then_inc(S["lgN_done"], 1)
                if back:
                    for t in range(H1T):
                        if t in (2, 3) and front:
                            pe.wait_ge(S["agg_lo_ready"], g.n(2, t - 1))
                        elif t >= 4:
                            pe.wait_ge(S["h1_relu_ready"], i.n(H1T, t - 3))
                        n = 0
                        for a, w in PARTS:
                            for f in range(FT):
                                mm = pe.matmul(bank[L1_BANKS[t]][:, 0:GN],
                                               wl1_hl[:, w, f, t * P:(t + 1) * P],
                                               (x1T_hi, x1T_lo)[a][:, f, :],
                                               start=n == 0, stop=n == 5)
                                n += 1
                        mm.then_inc(S["l1_done"], 1)
                    pe.wait_ge(S["gates_ready"], i.n(1, 1))
                    if front:
                        pe.wait_ge(S["deg_ready"], g.n(1, 1))
                    for s in range(NS):
                        mm = pe.transpose(bank[6][0:NB3, s * SP_:(s + 1) * SP_], wst[:, s, :],
                                          ident_sb[0:SP_, 0:SP_])
                    mm.then_inc(S["wT_done"], 1)

                def graph_layer(j):
                    for s in (2 * j, 2 * j + 1):
                        cols_ = slice(s * SP_, (s + 1) * SP_)
                        for b, hl, wt in ((4, (xT_hi, xT_lo), w1_hl), (2, (ag_hi, ag_lo), w2_hl)):
                            n = 0
                            o = bank[b + j][0:SP_, (s % 2) * D:(s % 2 + 1) * D]
                            for a, w in PARTS:
                                for f in range(FT):
                                    mm = pe.matmul(o, hl[a][:, f, cols_], wt[:, w, f, :],
                                                   start=n == 0, stop=n == 5)
                                    n += 1
                    mm.then_inc(S["gnn_done"], 1)

                if front:
                    pe.wait_ge(S["agg_lo_ready"], g.n(2, 2))
                    pe.wait_ge(S["xT_lo_ready"], g.n(2, 2))
                    if back:
                        pe.wait_ge(S["h1_relu_ready"], i.n(H1T, 4))
                    graph_layer(0)
                if back:
                    pe.wait_ge(S["wT_ready"], i.n(1, 1))
                    for t in range(2):
                        pe.matmul(bank[6 + t][:, 0:GN], selg_r[:, t, :], wT_r[:],
                                  start=True, stop=True).then_inc(S["gate_bc_done"], 1)
                    pe.wait_ge(S["h1_lo_ready"], i.n(H1T, H1T))
                    for t in range(H2T):
                        if t == 2:
                            pe.wait_ge(S["h2_relu_ready"], i.n(H2T, 1))
                        n = 0
                        for a, w in PARTS:
                            for e in range(2):
                                mm = pe.matmul(bank[t % 2][:, 0:GN], wl2_hl[:, w, 2 * t + e, :],
                                               (h1_hi, h1_lo)[a][:, 2 * t + e, :],
                                               start=n == 0, stop=n == 5)
                                n += 1
                        mm.then_inc(S["l2_done"], 1)
                if front:
                    graph_layer(1)
                if back:
                    pe.wait_ge(S["h2_lo_ready"], i.n(H2T, 2))
                    for s in range(NS):
                        cols_ = slice(s * SP_, (s + 1) * SP_)
                        o = bank[6 + s // 2][0:SP_, (s % 2) * D:(s % 2 + 1) * D]
                        pe.matmul(o, wT_r[:, cols_], b3_r[:], start=True, stop=False)
                        n = 0
                        for t in range(H2T):
                            if s == 0 and t == 2:
                                pe.wait_ge(S["h2_lo_ready"], i.n(H2T, H2T))
                            for a, w in PARTS:
                                mm = pe.matmul(o, (h2_hi, h2_lo)[a][:, t, cols_],
                                               wl3_hl[:, w, t, :], start=False,
                                               stop=n == 3 * H2T - 1)
                                n += 1
                        if s % 2:
                            mm.then_inc(S["l3_done"], 1)

            def step_scalar(act, i, more, front, back, prep):
                g, p = i + 1, i + 2

                def ag_high(f):
                    if f == 0 and g.c:
                        act.wait_ge(S["gnn_done"], g.n(2))
                    if more:
                        act.wait_ge(s_agf, g.n(FT, f + 1))
                        act.copy(ag_hi[:, f, :], agf_sb[:, f, :]).then_inc(S["agg_hi_ready"], 1)
                    else:
                        to_hi(act, ag_hi, g, f, 4 + f, "agg_done", "agg_hi_ready")
                if front:
                    ag_high(0)
                if back:
                    for f in range(FT):
                        to_hi(act, x1T_hi, i, f, f, "x1T_done", "x1T_hi_ready")
                if front:
                    ag_high(1)
                if back:
                    act.wait_ge(S["lg_done"], i.n(1, 1))
                    act.copy(lgT_sb[:], bank[7][0:8, 0:GN]).then_inc(S["lgT_ready"], 1)
                if front:
                    for f in range(FT):
                        to_hi(act, xT_hi, g, f, 2 + f, "xT_done", "xT_hi_ready")

                def h1_value(t):
                    act.wait_ge(S["l1_done"], i.n(H1T, t + 1))
                    if t >= NF1:
                        act.wait_ge(S["h1_lo_ready"], i.n(H1T, t + 1 - NF1))
                    elif i.c:
                        act.wait_ge(S["h1_lo_ready"], i.n(H1T))
                    act.activation(h1f[t % NF1][:], bank[L1_BANKS[t]][:, 0:GN], ACT.Relu,
                                   bias=bl1_sb[:, t:t + 1]).then_inc(S["h1_relu_ready"], 1)

                def h1_high(t):
                    act.wait_ge(S["h1_relu_ready"], i.n(H1T, t + 1))
                    if t == 0 and i.c:
                        act.wait_ge(S["l2_done"], i.n(H2T))
                    act.copy(h1_hi[:, t, :], h1f[t % NF1][:]).then_inc(S["h1_hi_ready"], 1)

                if back:
                    h1_value(0)
                    act.wait_ge(S["gate_step"], i.n(4, 3))
                    act.activation(ga[:], z[:], ACT.Exp).then_inc(S["exp_ready"], 1)
                    h1_value(1)
                    h1_high(0)
                    act.wait_ge(S["gate_step"], i.n(4, 4))
                    act.activation(gy[:], gd[:], ACT.Exp).then_inc(S["exp_ready"], 1)
                    for t in range(2, H1T):
                        h1_value(t)
                        h1_high(t - 1)
                    h1_high(H1T - 1)
                    act.wait_ge(S["wT_done"], i.n(1, 1))
                    act.copy(wT_r[:], bank[6][0:NB3, 0:GN]).then_inc(S["wT_ready"], 1)
                if prep:
                    edges_scalar_norm(act, p)
                if back:
                    def h2_value(t):
                        act.wait_ge(S["l2_done"], i.n(H2T, t + 1))
                        if i.c:
                            act.wait_ge(S["h2_lo_ready"], i.n(H2T))
                        act.activation(h2f[t][:], bank[t % 2][:, 0:GN], ACT.Relu,
                                       bias=bl2_sb[:, t:t + 1]).then_inc(S["h2_relu_ready"], 1)

                    def h2_high(t):
                        if t < 2:
                            act.wait_ge(S["h2_gated"], i.n(2, t + 1))
                        else:
                            act.wait_ge(S["h2_relu_ready"], i.n(H2T, H2T))
                        if i.c and t == 0:
                            act.wait_ge(S["l3_done"], i.n(2))
                        act.copy(h2_hi[:, t, :], h2f[t][:]).then_inc(S["h2_hi_ready"], 1)
                    h2_value(0)
                    h2_value(1)
                    h2_high(0)
                    h2_value(2)
                    h2_high(1)
                    h2_high(2)
                if prep:
                    edges_scalar_hi(act, p)
                    ln1_scalar(act, p)

            def gates_vector(dve, i):
                own = [0]
                NGS = 13

                def step(ins):
                    ins.then_inc(S["gates_own"], 1)
                    own[0] += 1
                    dve.wait_ge(S["gates_own"], i.n(NGS, own[0]))
                b4 = [SP_, NS, NX]
                dve.wait_ge(S["lgN_done"], i.n(1, 1))
                lg = bank[7][0:SP_, 0:NS * 8].rearrange("p (s k e) -> p s e k", s=NS, k=2)
                dve.tensor_reduce(z[:], lg, AX.X, ALU.add).then_inc(S["gate_step"], 1)
                dve.wait_ge(S["gate_step"], i.n(4, 1))
                dve.tensor_tensor(z[:], z[:], gb_sb[0:SP_].unsqueeze(1).to_broadcast(b4),
                                  ALU.add).then_inc(S["gate_step"], 1)
                dve.wait_ge(S["gate_step"], i.n(4, 2))
                step(dve.tensor_reduce(g1[:], z[:], AX.X, ALU.max))
                dve.tensor_tensor(z[:], z[:], g1[:].unsqueeze(2).to_broadcast(b4),
                                  ALU.subtract).then_inc(S["gate_step"], 1)
                dve.wait_ge(S["exp_ready"], i.n(2, 1))
                step(dve.tensor_reduce(g1[:], ga[:], AX.X, ALU.add))
                step(dve.reciprocal(g2[:], g1[:]))
                r = g2[:].unsqueeze(2).to_broadcast(b4)
                step(dve.tensor_tensor(ga[:], ga[:], r, ALU.mult))
                dve.tensor_tensor(gd[:], ga[:], r, ALU.subtract).then_inc(S["gate_step"], 1)
                b16 = [SP_, NS, NX, NX]
                step(dve.tensor_tensor(gpair[:], ga[:].unsqueeze(2).to_broadcast(b16),
                                       ga[:].unsqueeze(3).to_broadcast(b16), ALU.subtract))
                step(dve.tensor_tensor(gpair[:], gpair[:],
                                       tie_sb[0:SP_].unsqueeze(1).to_broadcast(b16), ALU.is_gt))
                step(dve.tensor_reduce(grank[:], gpair[:], AX.X, ALU.add))
                dve.wait_ge(S["exp_ready"], i.n(2, 2))
                step(dve.scalar_tensor_tensor(out=gd[:], in0=grank[:], scalar=1.5, in1=gy[:],
                                              op0=ALU.is_lt, op1=ALU.mult))
                step(dve.tensor_reduce(g1[:], gd[:], AX.X, ALU.add))
                step(dve.reciprocal(g2[:], g1[:]))
                if i.c:
                    dve.wait_ge(S["wT_done"], i.n(1))
                step(dve.tensor_tensor(gd[:], gd[:], r, ALU.mult))
                step(dve.tensor_copy(wst[:, :, 0:NX].bitcast(F32R), gd[:]))
                dve.tensor_copy(wst[:, :, 2 * NX:3 * NX].bitcast(F32R), gd[:])\
                   .then_inc(S["gates_own"], 1)
                dve.tensor_tensor(wst[:, :, NX:2 * NX], gd[:], wst[:, :, 0:NX],
                                  ALU.subtract).then_inc(S["gates_ready"], 1)
                assert own[0] + 1 == NGS

            def graph_vector(dve, g, j):
                dve.wait_ge(S["gnn_done"], g.n(2, j + 1))
                dve.tensor_tensor(
                    x1_sb[g.h][:, 2 * j:2 * j + 2, :],
                    bank[4 + j][0:SP_, :].rearrange("p (s d) -> p s d", s=2),
                    xb_sb[g.h][:, 2 * j:2 * j + 2, :], ALU.add).then_inc(S["t_ready"], 1)
                dve.wait_ge(S["t_ready"], g.n(2, j + 1))
                for s in (2 * j, 2 * j + 1):
                    dve.scalar_tensor_tensor(
                        out=x1_sb[g.h][:, s, :],
                        in0=bank[2 + j][0:SP_, (s % 2) * D:(s % 2 + 1) * D],
                        scalar=inv_deg[:, s:s + 1], in1=x1_sb[g.h][:, s, :],
                        op0=ALU.mult, op1=ALU.add).then_inc(S["x1_ready"], 1)

            def graph_stats(dve, g, j):
                L = ln[2]
                for s in (2 * j, 2 * j + 1):
                    dve.wait_ge(S["x1_ready"], g.n(NS, s + 1))
                    dve.bn_stats(L["st"][:, s, :], x1_sb[g.h][:, s, :])\
                       .then_inc(S["l2_st_ready"], 1)

            def step_vector(dve, i, more, front, back, prep):
                g, p = i + 1, i + 2

                def ag_low(f):
                    if more:
                        dve.wait_ge(S["agg_hi_ready"], g.n(2, f + 1))
                        dve.tensor_tensor(ag_lo[:, f, :], agf_sb[:, f, :],
                                          ag_hi[:, f, :].bitcast(F32),
                                          ALU.subtract).then_inc(S["agg_lo_ready"], 1)
                    else:
                        to_lo(dve, ag_lo, ag_hi, g, f, 4 + f, "agg_hi_ready", "agg_lo_ready")

                def add_more(f):
                    dve.wait_ge(s_more, g.n(32, 32))
                    dve.wait_ge(S["agg_done"], g.n(3, f + 1))
                    dve.tensor_tensor(agf_sb[:, f, :], bank[4 + f][:, 0:GN],
                                      more_sb[:, f, :], ALU.add).then_inc(s_agf, 1)
                if front:
                    if more:
                        add_more(0)
                    ag_low(0)
                if back:
                    for f in range(FT):
                        to_lo(dve, x1T_lo, x1T_hi, i, f, f, "x1T_hi_ready", "x1T_lo_ready")
                if prep:
                    edges_vector_a(dve, p)
                if front:
                    if more:
                        add_more(1)
                        dve.wait_ge(S["agg_done"], g.n(3, 3))
                        dve.tensor_tensor(cnt_sb[:], bank[6][0:SP_, 0:NS], more_cnt[:],
                                          ALU.add).then_inc(S["cnt_ready"], 1)
                    ag_low(1)
                    for f in range(FT):
                        to_lo(dve, xT_lo, xT_hi, g, f, 2 + f, "xT_hi_ready", "xT_lo_ready")
                    dve.wait_ge(S["agg_done"], g.n(3, 3))
                    if more:
                        dve.wait_ge(S["cnt_ready"], g.n(1, 1))
                    dve.tensor_scalar(deg[:], cnt_sb[:] if more else bank[6][0:SP_, 0:NS], 1.0,
                                      None, ALU.max).then_inc(S["deg_ready"], 1)
                    dve.wait_ge(S["deg_ready"], g.n(1, 1))
                    dve.reciprocal(inv_deg[:], deg[:]).then_inc(S["inv_ready"], 1)

                def h1_low(t):
                    dve.wait_ge(S["h1_hi_ready"], i.n(H1T, t + 1))
                    dve.tensor_tensor(h1_lo[:, t, :], h1f[t % NF1][:],
                                      h1_hi[:, t, :].bitcast(F32),
                                      ALU.subtract).then_inc(S["h1_lo_ready"], 1)
                if back:
                    gates_vector(dve, i)
                if prep:
                    edges_vector_nb(dve, p)
                if back:
                    for t in range(H1T):
                        h1_low(t)
                if prep:
                    ln1_vector_a(dve, p)
                if front:
                    dve.wait_ge(S["xb_ready"], g.n(1, 1))
                    dve.wait_ge(S["inv_ready"], g.n(1, 1))
                    graph_vector(dve, g, 0)

                def gated(t):
                    dve.wait_ge(S["gate_bc_done"], i.n(2, t + 1))
                    dve.wait_ge(S["h2_relu_ready"], i.n(H2T, t + 1))
                    dve.tensor_tensor(h2f[t][:], h2f[t][:], bank[6 + t][:, 0:GN],
                                      ALU.mult).then_inc(S["h2_gated"], 1)

                def h2_low(t):
                    dve.wait_ge(S["h2_hi_ready"], i.n(H2T, t + 1))
                    dve.tensor_tensor(h2_lo[:, t, :], h2f[t][:], h2_hi[:, t, :].bitcast(F32),
                                      ALU.subtract).then_inc(S["h2_lo_ready"], 1)
                if back:
                    gated(0)
                if front:
                    if g.c:
                        dve.wait_ge(S["l2_var_ready"], g.n(1))
                    graph_stats(dve, g, 0)
                if back:
                    gated(1)
                    for t in range(H2T):
                        h2_low(t)
                if prep:
                    ln1_vector_nb(dve, p)
                if front:
                    L = ln[2]
                    graph_vector(dve, g, 1)
                    graph_stats(dve, g, 1)
                    for s in range(NS):
                        wait_alone(dve, S["l2_st_ready"], g.n(NS, s + 1))
                        dve.bn_aggr(L["mv"][:, s, :], L["st"][:, s, :])\
                           .then_inc(S["l2_mv_ready"], 1)
                if prep:
                    edges_vector_lo(dve, p)
                if front:
                    dve.wait_ge(S["l2_rstd_ready"], g.n(1, 1))
                    if g.c:
                        dve.wait_ge(S["x1T_done"], g.n(2))
                    for s in range(NS):
                        dve.tensor_scalar(x1n_sb[:, s, :], x1_sb[g.h][:, s, :],
                                          L["mv"][:, s, 0:1], L["rstd"][:, s:s + 1],
                                          ALU.subtract, ALU.mult).then_inc(S["x1n_ready"], 1)
                if back:
                    if i.c >= 2:
                        dve.wait_ge(s_store[i.h], (i + -2).dma(16))
                    for j in range(2):
                        dve.wait_ge(S["l3_done"], i.n(2, j + 1))
                        dve.tensor_tensor(
                            out_sb[i.h][:, 2 * j:2 * j + 2, :],
                            bank[6 + j][0:SP_, :].rearrange("p (s d) -> p s d", s=2),
                            x1_sb[i.h][:, 2 * j:2 * j + 2, :], ALU.add).then_inc(S["out_ready"], 1)

            def load_x(sp, g):
                if g.c >= 2:
                    sp.wait_ge(S["l1_st_ready"], g.n(NS, -NS))
                    sp.wait_ge(S["xn_ready"], g.n(NS, -NS))
                    sp.wait_ge(S["xb_ready"], g.n(1, -1))
                sp.dma_start(x_sb[g.h][:], x_v[bass.ds(g.at(), 1)][0] if not isinstance(g.k, int)
                             else x_v[g.at()]).then_inc(s_x[g.h], 16)

            def load_more(sp, g):
                if g.c:
                    sp.wait_ge(s_agf, g.n(FT))
                    sp.wait_ge(S["cnt_ready"], g.n(1))
                at = bass.ds(g.at(), 1)
                if isinstance(g.k, int):
                    at = slice(g.at(), g.at() + 1)
                sp.dma_start(more_sb[:].rearrange("p f n -> p (f n)"), agg_x[at][0])\
                  .then_inc(s_more, 16)
                sp.dma_start(more_cnt[:], cnt_x[at][0]).then_inc(s_more, 16)

            def step_sync(sp, i, more, back, load):
                if load:
                    load_x(sp, i + 3)
                if more and (not isinstance(i.k, int) or i.c + 2 < NG):
                    load_more(sp, i + 2)
                if back:
                    sp.wait_ge(S["out_ready"], i.n(2, 2))
                    sp.dma_start(out_v[bass.ds(i.at(), 1)][0] if not isinstance(i.k, int)
                                 else out_v[i.at()], out_sb[i.h][:]).then_inc(s_store[i.h], 16)

            def step_pool(pool, i, front, prep, load):
                if load:
                    gather(pool, i + 3)
                if prep:
                    layernorm_pool(pool, i + 2, 0, e_mv, "e", EQ)
                    edges_pool_oh(pool, i + 2)
                    edges_pool_sum(pool, i + 2)
                    layernorm_pool(pool, i + 2, 1, ln[1]["mv"], "l1", NS)
                if front:
                    layernorm_pool(pool, i + 1, 2, ln[2]["mv"], "l2", NS)
                if prep:
                    xb_pool(pool, i + 2)

            def steps(run, eng):
                run(eng, G(0, -1))
                run(eng, G(0, 0))
                run(eng, G(0, 1))
                run(eng, G(0, 2))
                with eng.Fori(0, (NG - 6) // 2) as k:
                    run(eng, G(k, 3))
                    run(eng, G(k, 4))
                for c in range(NG - 3, NG):
                    run(eng, G(0, c))

            def flags(i):
                if not isinstance(i.k, int):
                    return dict(front=True, back=True, prep=True, load=True)
                return dict(front=i.c + 1 < NG, back=i.c >= 0, prep=i.c + 2 < NG,
                            load=i.c + 3 < NG)

            def either(eng, program):
                rounds = eng.value_load(rounds_sb[0:1, 0:1], min_val=1, max_val=E // CAP + 1)
                with eng.If(rounds < 2):
                    program(False)
                with eng.If(rounds > 1):
                    program(True)

            with nc.Block() as block:
                @block.sync
                def _(sp):
                    def program(more):
                        load_x(sp, G(0, 0))
                        load_x(sp, G(0, 1))
                        if more:
                            load_more(sp, G(0, 0))

                        def run(e, i):
                            f = flags(i)
                            step_sync(e, i, more, f["back"], f["load"])
                        steps(run, sp)
                        for h in range(2):
                            sp.wait_ge(s_store[h], 16 * (NG // 2))
                    either(sp, program)

                @block.gpsimd
                def _(pool):
                    pool.wait_ge(S["rows_cleared"], 2)
                    gather(pool, G(0, 0))
                    gather(pool, G(0, 1))
                    layernorm_pool(pool, G(0, 0), 0, e_mv, "e", EQ)
                    layernorm_pool(pool, G(0, 0), 1, ln[1]["mv"], "l1", NS)
                    edges_pool_oh(pool, G(0, 0))
                    edges_pool_sum(pool, G(0, 0))
                    xb_pool(pool, G(0, 0))

                    def run(e, i):
                        f = flags(i)
                        step_pool(e, i, f["front"], f["prep"], f["load"])
                    steps(run, pool)

                @block.vector
                def _(dve):
                    for h in range(2):
                        dve.memset(rows[h][:], 0.0).then_inc(S["rows_cleared"], 1)
                    dve.memset(wst[:], 1.0).then_inc(S["rows_cleared"], 1)
                    dve.memset(one16[:], 1.0).then_inc(S["rows_cleared"], 1)
                    dve.wait_ge(S["rows_cleared"], 4)

                    def program(more):
                        p = G(0, 0)
                        edges_vector_a(dve, p)
                        ln1_vector_a(dve, p)
                        edges_vector_nb(dve, p)
                        ln1_vector_nb(dve, p)
                        edges_vector_lo(dve, p)

                        def run(e, i):
                            f = flags(i)
                            step_vector(e, i, more, f["front"], f["back"], f["prep"])
                        steps(run, dve)
                    either(dve, program)

                @block.scalar
                def _(act):
                    def program(more):
                        edges_scalar_norm(act, G(0, 0))
                        edges_scalar_hi(act, G(0, 0))
                        ln1_scalar(act, G(0, 0))

                        def run(e, i):
                            f = flags(i)
                            step_scalar(e, i, more, f["front"], f["back"], f["prep"])
                        steps(run, act)
                    either(act, program)

                @block.tensor
                def _(pe):
                    pe.wait_ge(S["rows_cleared"], 4)

                    def run(e, i):
                        f = flags(i)
                        step_tensor(e, i, f["front"], f["back"])
                    steps(run, pe)


def _rows(a):
    return np.ascontiguousarray(a)


def kernel(**inputs):
    import concourse.bacc as bacc
    from concourse.bass_utils import run_bass_kernel_spmd

    v = {k: np.asarray(a) for k, a in inputs.items()}
    f = "L0_ffn_"

    def tiles(w):
        return _rows(w.reshape(w.shape[0] // P, P, w.shape[1]).transpose(1, 0, 2))

    e1 = v[f + "eW1"]
    l1 = np.concatenate([e1[e] for e in range(NX)] + [v[f + "sW1"]], axis=1)
    e2 = v[f + "eW2"]
    half = np.zeros_like(e2[0])
    l2 = np.stack([np.concatenate([e2[e], half] if e % 2 == 0 else [half, e2[e]], axis=1)
                   for e in range(NX)] + [v[f + "sW2"][0:P], v[f + "sW2"][P:2 * P]], axis=1)
    l3 = np.concatenate([v[f + "eW3"].reshape(NX * 64, D), v[f + "sW3"]], axis=0)
    b1 = np.concatenate([v[f + "eb1"].reshape(-1), v[f + "sb1"]]).reshape(H1T, P).T
    b2 = np.concatenate([v[f + "eb2"].reshape(-1), v[f + "sb2"]]).reshape(H2T, P).T
    b3 = np.concatenate([v[f + "eb3"]] * 3 + [v[f + "sb3"][None]] * 2, axis=0)

    selg = np.zeros((NB3, 3, P), np.float32)
    for e in range(NX):
        for k in range(2):
            selg[k * NX + e, e // 2, (e % 2) * 64:(e % 2) * 64 + 64] = 1
    low = np.array([0] * 8 + [1] * 4 + [0, 1])
    selg[:, 2, 0] = 1 - low
    selg[:, 2, 1] = low
    tie = np.zeros((P, NX, NX), np.float32)
    for e in range(NX):
        tie[:, e, :e] = -1.1754944e-38
    bases16 = np.zeros((EP + 1, EP + 1), np.float16)
    bases16[0, :EP] = LOW
    bases16[EP, :] = 1
    named = {
        "x": v["x"], "src": v["src"].reshape(EP, EC), "dst": v["dst"].reshape(EP, EC),
        "w1t": tiles(v["L0_gnn_W1"].T), "w2t": tiles(v["L0_gnn_W2"].T),
        "b12": np.stack([v["L0_gnn_b1"], v["L0_gnn_b2"]]),
        "wl1": tiles(l1), "bl1": b1, "wl2": l2, "bl2": b2, "wl3": tiles(l3), "b3": b3,
        "gw": tiles(v[f + "gW"]), "gb": v[f + "gb"],
        "ident": np.eye(P, dtype=np.float32),
        "bases16": bases16,
        "upper16": np.triu(np.ones((EP, EP + 1)), 1).astype(np.float16),
        "iota16": np.tile(np.arange(GN), (P, 1)).astype(np.float16),
        "iota": np.tile(np.arange(1, GN + 1), (P, 1)).astype(np.float32),
        "selg": selg, "tie": tie,
    }
    nc = bacc.Bacc("TRN2", target_bir_lowering=False, num_devices=1)
    arrays, args = {}, {}
    for name, a in named.items():
        a = _rows(a)
        arrays["in_" + name] = a
        args[name] = nc.dram_tensor("in_" + name, a.shape, mybir.dt.from_np(a.dtype),
                                    kind="ExternalInput").ap()
    out = nc.dram_tensor("out", (N, D), F32, kind="ExternalOutput").ap()
    agg_x = nc.dram_tensor("agg_x", (NG, P, FT * GN), F32, kind="Internal").ap()
    cnt_x = nc.dram_tensor("cnt_x", (NG, SP_, NS), F32, kind="Internal").ap()
    build(nc, out=out, agg_x=agg_x, cnt_x=cnt_x, **args)
    return run_bass_kernel_spmd(nc, [arrays], core_ids=[0]).results[0]["out"]
```
